# Optimizing a Trainium2 kernel written in Bass

```python
import numpy as np
import jax
import jax.numpy as jnp

def _softmax(x, axis=-1):
    return jax.nn.softmax(x, axis=axis)

def _gelu(x):
    return jax.nn.gelu(x, approximate=True)

def _silu(x):
    return jax.nn.silu(x)

def _sigmoid(x):
    return jax.nn.sigmoid(x)

def _layernorm(x, axis=-1, eps=1e-05):
    m = jnp.mean(x, axis=axis, keepdims=True)
    v = jnp.var(x, axis=axis, keepdims=True)
    return (x - m) / jnp.sqrt(v + eps)

def _scatter_add(tgt, idx, src, axis=0):
    return tgt.at[idx].add(src)

def _segment_sum(src, seg, n):
    return jax.ops.segment_sum(src, seg, n)
kernel_name = 'mk_adaln_d1_jaxref_r4_29dfa2'

def setup_inputs(seed: int=0):
    np.random.seed(seed)
    _w = jnp.asarray

    def _L0_attn_setup():
        import jax, jax.numpy as jnp
        import numpy as np
        NUM_HEADS = 16
        HIDDEN = 256
        ATTN_DIM = 64
        HEAD_OUT = 64
        OUT_DIM = 256
        BATCH, SEQ = (2, 512)

        def _split_heads(y, h):
            b, s, _ = y.shape
            return y.reshape(b, s, h, -1).transpose(0, 2, 1, 3)
        key = jax.random.key(seed)
        ks = jax.random.split(key, 9)
        s_in = 1.0 / np.sqrt(HIDDEN)
        s_o = 1.0 / np.sqrt(NUM_HEADS * HEAD_OUT)
        return {'x': jax.random.normal(ks[0], (BATCH, SEQ, HIDDEN), dtype=jnp.float32), 'Wq': jax.random.uniform(ks[1], (HIDDEN, NUM_HEADS * ATTN_DIM), jnp.float32, -s_in, s_in), 'bq': jax.random.uniform(ks[2], (NUM_HEADS * ATTN_DIM,), jnp.float32, -s_in, s_in), 'Wk': jax.random.uniform(ks[3], (HIDDEN, NUM_HEADS * ATTN_DIM), jnp.float32, -s_in, s_in), 'bk': jax.random.uniform(ks[4], (NUM_HEADS * ATTN_DIM,), jnp.float32, -s_in, s_in), 'Wv': jax.random.uniform(ks[5], (HIDDEN, NUM_HEADS * HEAD_OUT), jnp.float32, -s_in, s_in), 'bv': jax.random.uniform(ks[6], (HIDDEN, NUM_HEADS * HEAD_OUT)[1:], jnp.float32, -s_in, s_in), 'Wo': jax.random.uniform(ks[7], (NUM_HEADS * HEAD_OUT, OUT_DIM), jnp.float32, -s_o, s_o), 'bo': jax.random.uniform(ks[8], (OUT_DIM,), jnp.float32, -s_o, s_o)}
    _L0_attn_in = _L0_attn_setup()

    def _L0_ffn_setup():
        import jax, jax.numpy as jnp
        import numpy as np
        DIM = 256
        DEPTH = 2
        HEADS = 8
        DIM_HEAD = 64
        WINDOW = 128
        INNER = HEADS * DIM_HEAD
        HID = int(DIM * 4 * 2 / 3)
        B, N = (2, 2048)
        QK_SCALE = 8.0

        def shift_token(t):
            t1, t2 = jnp.split(t, 2, axis=-1)
            t2 = jnp.pad(t2, ((0, 0), (1, 0), (0, 0)))[:, :-1]
            return jnp.concatenate([t1, t2], axis=-1)

        def l2norm(t):
            return t / jnp.clip(jnp.linalg.norm(t, axis=-1, keepdims=True), 1e-12)

        def rotate_half(x):
            x1, x2 = jnp.split(x, 2, axis=-1)
            return jnp.concatenate([-x2, x1], axis=-1)

        def rotary_xpos(q, k):
            n = q.shape[-2]
            half_idx = jnp.arange(0, DIM_HEAD, 2, dtype=jnp.float32)
            inv_freq = 1.0 / 10000.0 ** (half_idx / DIM_HEAD)
            t = jnp.arange(n, dtype=jnp.float32)
            freqs = t[:, None] * inv_freq[None, :]
            freqs = jnp.concatenate([freqs, freqs], axis=-1)
            base = (half_idx + 0.4 * DIM_HEAD) / (1.4 * DIM_HEAD)
            power = (t - n // 2) / float(WINDOW // 2)
            scale = base[None, :] ** power[:, None]
            scale = jnp.concatenate([scale, scale], axis=-1)
            cos, sin = (jnp.cos(freqs), jnp.sin(freqs))
            q = q * cos * scale + rotate_half(q) * sin * scale
            k = k * cos / scale + rotate_half(k) * sin / scale
            return (q, k)

        def local_attention(q, k, v):
            b, h, n, d = q.shape
            w = n // WINDOW
            bq = q.reshape(b, h, w, WINDOW, d) * QK_SCALE
            bk = k.reshape(b, h, w, WINDOW, d)
            bv = v.reshape(b, h, w, WINDOW, d)

            def look_around(t):
                p = jnp.pad(t, ((0, 0), (0, 0), (1, 0), (0, 0), (0, 0)))
                return jnp.concatenate([p[:, :, :w], p[:, :, 1:]], axis=3)
            bk, bv = (look_around(bk), look_around(bv))
            bt = jnp.arange(n).reshape(w, WINDOW)
            btp = jnp.pad(bt, ((1, 0), (0, 0)), constant_values=-1)
            btk = jnp.concatenate([btp[:w], btp[1:]], axis=1)
            sim = jnp.einsum('bhwid,bhwjd->bhwij', bq, bk)
            i = bt[:, :, None]
            j = btk[:, None, :]
            mask = (i < j) | (i > j + WINDOW) | (j == -1)
            sim = jnp.where(mask, -jnp.finfo(sim.dtype).max, sim)
            attn = jax.nn.softmax(sim, axis=-1)
            out = jnp.einsum('bhwij,bhwjd->bhwid', attn, bv)
            return out.reshape(b, h, n, d)

        def _layer(x, wqkv, qs, ksc, wo, lg, lb, w1, b1, w2, b2):
            b, n, _ = x.shape
            h = shift_token(x)
            qkv = h @ wqkv
            q, k, v = jnp.split(qkv, 3, axis=-1)
            to_heads = lambda t: t.reshape(b, n, HEADS, DIM_HEAD).transpose(0, 2, 1, 3)
            q, k, v = (to_heads(q), to_heads(k), to_heads(v))
            q = l2norm(q) * qs
            k = l2norm(k) * ksc
            q, k = rotary_xpos(q, k)
            o = local_attention(q, k, v)
            o = o.transpose(0, 2, 1, 3).reshape(b, n, INNER)
            x = x + o @ wo
            h = shift_token(x)
            mu = h.mean(-1, keepdims=True)
            var = h.var(-1, keepdims=True)
            h = (h - mu) / jnp.sqrt(var + 1e-05) * lg + lb
            h = h @ w1 + b1
            a, g = jnp.split(h, 2, axis=-1)
            h = a * jax.nn.gelu(g, approximate=False)
            x = x + h @ w2 + b2
            return x
        key = jax.random.key(seed)
        ks = jax.random.split(key, 6)
        return {'x': jax.random.normal(ks[0], (B, N, DIM), jnp.float32), 'wqkv': jax.random.normal(ks[1], (DEPTH, DIM, 3 * INNER), jnp.float32) * 0.02, 'q_scale': jnp.ones((DEPTH, DIM_HEAD), jnp.float32), 'k_scale': jnp.ones((DEPTH, DIM_HEAD), jnp.float32), 'wo': jax.random.normal(ks[2], (DEPTH, INNER, DIM), jnp.float32) * 0.02, 'ln_g': jnp.ones((DEPTH, DIM), jnp.float32), 'ln_b': jnp.zeros((DEPTH, DIM), jnp.float32), 'w1': jax.random.normal(ks[3], (DEPTH, DIM, 2 * HID), jnp.float32) * 0.02, 'b1': jnp.zeros((DEPTH, 2 * HID), jnp.float32), 'w2': jax.random.normal(ks[4], (DEPTH, HID, DIM), jnp.float32) * 0.02, 'b2': jnp.zeros((DEPTH, DIM), jnp.float32)}
    _L0_ffn_in = _L0_ffn_setup()
    _L0_c = _w((lambda *s: np.random.randn(*s).astype(np.float32) * 0.05)(2, 256))
    _L0_wmod = _w((lambda *s: np.random.randn(*s).astype(np.float32) * 0.05)(256, 6 * 256) * 256 ** (-0.5))
    _d = {'L0_attn_x': _L0_attn_in['x'], 'L0_attn_Wq': _L0_attn_in['Wq'], 'L0_attn_bq': _L0_attn_in['bq'], 'L0_attn_Wk': _L0_attn_in['Wk'], 'L0_attn_bk': _L0_attn_in['bk'], 'L0_attn_Wv': _L0_attn_in['Wv'], 'L0_attn_bv': _L0_attn_in['bv'], 'L0_attn_Wo': _L0_attn_in['Wo'], 'L0_attn_bo': _L0_attn_in['bo'], 'L0_ffn_wqkv': _L0_ffn_in['wqkv'], 'L0_ffn_q_scale': _L0_ffn_in['q_scale'], 'L0_ffn_k_scale': _L0_ffn_in['k_scale'], 'L0_ffn_wo': _L0_ffn_in['wo'], 'L0_ffn_ln_g': _L0_ffn_in['ln_g'], 'L0_ffn_ln_b': _L0_ffn_in['ln_b'], 'L0_ffn_w1': _L0_ffn_in['w1'], 'L0_ffn_b1': _L0_ffn_in['b1'], 'L0_ffn_w2': _L0_ffn_in['w2'], 'L0_ffn_b2': _L0_ffn_in['b2'], 'L0_c': _L0_c, 'L0_wmod': _L0_wmod}
    _x0 = _d['L0_attn_x']
    _d['L0_attn_x'] = jax.random.normal(jax.random.fold_in(jax.random.key(seed), 1), (2, 2048, 256), dtype=_x0.dtype)
    del _x0
    return _d

def reference(L0_attn_x, L0_attn_Wq, L0_attn_bq, L0_attn_Wk, L0_attn_bk, L0_attn_Wv, L0_attn_bv, L0_attn_Wo, L0_attn_bo, L0_ffn_wqkv, L0_ffn_q_scale, L0_ffn_k_scale, L0_ffn_wo, L0_ffn_ln_g, L0_ffn_ln_b, L0_ffn_w1, L0_ffn_b1, L0_ffn_w2, L0_ffn_b2, L0_c, L0_wmod):

    def _L0_attn_ref(x, Wq, bq, Wk, bk, Wv, bv, Wo, bo):
        import jax, jax.numpy as jnp
        import numpy as np
        NUM_HEADS = 16
        HIDDEN = 256
        ATTN_DIM = 64
        HEAD_OUT = 64
        OUT_DIM = 256
        BATCH, SEQ = (2, 512)

        def _split_heads(y, h):
            b, s, _ = y.shape
            return y.reshape(b, s, h, -1).transpose(0, 2, 1, 3)
        h = NUM_HEADS
        q = _split_heads(x @ Wq + bq, h)
        k = _split_heads(x @ Wk + bk, h)
        v = _split_heads(x @ Wv + bv, h)
        scale = 1.0 / jnp.sqrt(jnp.float32(ATTN_DIM))
        pattern = jnp.einsum('bhid,bhjd->bhij', k, q) * scale
        prob = jax.nn.softmax(pattern, axis=-2)
        out = jnp.einsum('bhis,bhid->bhsd', prob, v)
        b, _, s, dv = out.shape
        concat = out.transpose(0, 2, 1, 3).reshape(b, s, h * dv)
        return concat @ Wo + bo

    def _L0_ffn_ref(x, wqkv, q_scale, k_scale, wo, ln_g, ln_b, w1, b1, w2, b2):
        import jax, jax.numpy as jnp
        import numpy as np
        DIM = 256
        DEPTH = 2
        HEADS = 8
        DIM_HEAD = 64
        WINDOW = 128
        INNER = HEADS * DIM_HEAD
        HID = int(DIM * 4 * 2 / 3)
        B, N = (2, 2048)
        QK_SCALE = 8.0

        def shift_token(t):
            t1, t2 = jnp.split(t, 2, axis=-1)
            t2 = jnp.pad(t2, ((0, 0), (1, 0), (0, 0)))[:, :-1]
            return jnp.concatenate([t1, t2], axis=-1)

        def l2norm(t):
            return t / jnp.clip(jnp.linalg.norm(t, axis=-1, keepdims=True), 1e-12)

        def rotate_half(x):
            x1, x2 = jnp.split(x, 2, axis=-1)
            return jnp.concatenate([-x2, x1], axis=-1)

        def rotary_xpos(q, k):
            n = q.shape[-2]
            half_idx = jnp.arange(0, DIM_HEAD, 2, dtype=jnp.float32)
            inv_freq = 1.0 / 10000.0 ** (half_idx / DIM_HEAD)
            t = jnp.arange(n, dtype=jnp.float32)
            freqs = t[:, None] * inv_freq[None, :]
            freqs = jnp.concatenate([freqs, freqs], axis=-1)
            base = (half_idx + 0.4 * DIM_HEAD) / (1.4 * DIM_HEAD)
            power = (t - n // 2) / float(WINDOW // 2)
            scale = base[None, :] ** power[:, None]
            scale = jnp.concatenate([scale, scale], axis=-1)
            cos, sin = (jnp.cos(freqs), jnp.sin(freqs))
            q = q * cos * scale + rotate_half(q) * sin * scale
            k = k * cos / scale + rotate_half(k) * sin / scale
            return (q, k)

        def local_attention(q, k, v):
            b, h, n, d = q.shape
            w = n // WINDOW
            bq = q.reshape(b, h, w, WINDOW, d) * QK_SCALE
            bk = k.reshape(b, h, w, WINDOW, d)
            bv = v.reshape(b, h, w, WINDOW, d)

            def look_around(t):
                p = jnp.pad(t, ((0, 0), (0, 0), (1, 0), (0, 0), (0, 0)))
                return jnp.concatenate([p[:, :, :w], p[:, :, 1:]], axis=3)
            bk, bv = (look_around(bk), look_around(bv))
            bt = jnp.arange(n).reshape(w, WINDOW)
            btp = jnp.pad(bt, ((1, 0), (0, 0)), constant_values=-1)
            btk = jnp.concatenate([btp[:w], btp[1:]], axis=1)
            sim = jnp.einsum('bhwid,bhwjd->bhwij', bq, bk)
            i = bt[:, :, None]
            j = btk[:, None, :]
            mask = (i < j) | (i > j + WINDOW) | (j == -1)
            sim = jnp.where(mask, -jnp.finfo(sim.dtype).max, sim)
            attn = jax.nn.softmax(sim, axis=-1)
            out = jnp.einsum('bhwij,bhwjd->bhwid', attn, bv)
            return out.reshape(b, h, n, d)

        def _layer(x, wqkv, qs, ksc, wo, lg, lb, w1, b1, w2, b2):
            b, n, _ = x.shape
            h = shift_token(x)
            qkv = h @ wqkv
            q, k, v = jnp.split(qkv, 3, axis=-1)
            to_heads = lambda t: t.reshape(b, n, HEADS, DIM_HEAD).transpose(0, 2, 1, 3)
            q, k, v = (to_heads(q), to_heads(k), to_heads(v))
            q = l2norm(q) * qs
            k = l2norm(k) * ksc
            q, k = rotary_xpos(q, k)
            o = local_attention(q, k, v)
            o = o.transpose(0, 2, 1, 3).reshape(b, n, INNER)
            x = x + o @ wo
            h = shift_token(x)
            mu = h.mean(-1, keepdims=True)
            var = h.var(-1, keepdims=True)
            h = (h - mu) / jnp.sqrt(var + 1e-05) * lg + lb
            h = h @ w1 + b1
            a, g = jnp.split(h, 2, axis=-1)
            h = a * jax.nn.gelu(g, approximate=False)
            x = x + h @ w2 + b2
            return x
        for l in range(DEPTH):
            x = _layer(x, wqkv[l], q_scale[l], k_scale[l], wo[l], ln_g[l], ln_b[l], w1[l], b1[l], w2[l], b2[l])
        return x
    x = L0_attn_x
    mod = (_silu(L0_c) @ L0_wmod).reshape(L0_c.shape[0], 6, 1, -1)
    sa, ca, ga, sb, cb, gb = (mod[:, 0], mod[:, 1], mod[:, 2], mod[:, 3], mod[:, 4], mod[:, 5])
    ga = (2 * (ga >= 0) - 1) * jnp.maximum(jnp.abs(ga), 0.25)
    gb = (2 * (gb >= 0) - 1) * jnp.maximum(jnp.abs(gb), 0.25)
    h = _layernorm(x, axis=-1) * (1 + ca) + sa
    x = x + ga * _L0_attn_ref(h, L0_attn_Wq, L0_attn_bq, L0_attn_Wk, L0_attn_bk, L0_attn_Wv, L0_attn_bv, L0_attn_Wo, L0_attn_bo)
    h = _layernorm(x, axis=-1) * (1 + cb) + sb
    x = x + gb * _L0_ffn_ref(h, L0_ffn_wqkv, L0_ffn_q_scale, L0_ffn_k_scale, L0_ffn_wo, L0_ffn_ln_g, L0_ffn_ln_b, L0_ffn_w1, L0_ffn_b1, L0_ffn_w2, L0_ffn_b2)
    return x

_drawn_inputs = setup_inputs


def setup_inputs(seed=0):
    import zlib

    import numpy as np

    out = dict(_drawn_inputs(seed))
    spreads = {'L0_ffn_q_scale': (1.0, 0.6),
     'L0_ffn_k_scale': (1.0, 0.6),
     'L0_ffn_ln_g': (1.0, 0.6),
     'L0_ffn_ln_b': (0.0, 0.8),
     'L0_ffn_b1': (0.0, 0.8),
     'L0_ffn_b2': (0.0, 0.505)}
    factors = {'L0_attn_Wq': 8.0,
     'L0_attn_bq': 8.0,
     'L0_attn_Wk': 8.0,
     'L0_attn_bk': 64.0,
     'L0_attn_Wv': 8.0,
     'L0_attn_bv': 8.0,
     'L0_attn_Wo': 8.0,
     'L0_attn_bo': 8.0,
     'L0_ffn_wqkv': 7.461,
     'L0_ffn_wo': 7.283,
     'L0_ffn_w1': 4.789,
     'L0_ffn_w2': 4.774}
    for name, (base, spread) in spreads.items():
        noise = np.random.default_rng([zlib.crc32(name.encode()), seed]).standard_normal(out[name].shape)
        drawn = base * np.exp(spread * noise) if base else spread * noise
        out[name] = jnp.asarray(drawn.astype(out[name].dtype))
    for name, factor in factors.items():
        out[name] = (out[name] * factor).astype(out[name].dtype)
    return out
```

```python
from contextlib import ExitStack

import numpy as np

import concourse.bass as bass
from concourse import mybir

F32 = mybir.dt.float32
F32R = mybir.dt.float32r
BF16 = mybir.dt.bfloat16
ALU = mybir.AluOpType
ACT = mybir.ActivationFunctionType
AX_X = mybir.AxisListType.X

P = 128
B, N, D = 2, 2048, 256
HALVES = D // P
T = 512
CHUNKS = N // T
EPS = 1e-5

HEADS, DH = 16, 64
PAIRS = HEADS // 2
KT = N // P
CP = CHUNKS // 2
STEPS = CP * KT
PRING = 4
SUM_DVE = (4, 9, 14)
SUM_POOL = tuple(k for k in range(KT) if k not in SUM_DVE)
POOL_OPS = len(SUM_POOL) - 1
DVE_OPS = len(SUM_DVE)
QK_ITEMS, V_ITEMS = CHUNKS, 2
PJ_ITEMS = QK_ITEMS + V_ITEMS
WO_ITEMS = CHUNKS * HALVES
RING_MAX = KT * CHUNKS
RING_PAIR = 2 * (RING_MAX + 1 + CP) + WO_ITEMS
ATT_SCALE = 1.0 / np.sqrt(np.float32(DH))

LAYERS, LHEADS, WIN = 2, 8, 128
INNER = LHEADS * DH
LPAIRS = LHEADS // 2
WINDOWS = N // WIN
ITEMS = 2
IH = LHEADS // ITEMS
HID = int(D * 4 * 2 / 3)
HID_TILES = [(o, min(P, HID - o)) for o in range(0, HID, P)]
HT = len(HID_TILES)
QK_SCALE = 8.0
MASKED = -1.0e30


def shape_constants():
    f = np.float32
    eye = np.eye(P, dtype=f)
    half = np.arange(0, DH, 2, dtype=f)
    inv = (f(1.0) / np.power(f(10000.0), half / f(DH))).astype(f)
    t = np.arange(N, dtype=f)
    fr = (t[:, None] * inv[None, :]).astype(f)
    fr = np.concatenate([fr, fr], -1)
    base = ((half + f(0.4 * DH)) / f(1.4 * DH)).astype(f)
    power = ((t - N // 2) / f(WIN // 2)).astype(f)
    sc = np.power(base[None, :].astype(np.float64), power[:, None].astype(np.float64)).astype(f)
    sc = np.concatenate([sc, sc], -1)
    cos, sin = np.cos(fr.astype(np.float64)).astype(f), np.sin(fr.astype(np.float64)).astype(f)
    sign = np.concatenate([-np.ones(DH // 2, f), np.ones(DH // 2, f)])
    tabs = [cos * sc, sin * sc * sign, cos / sc, sin / sc * sign]
    rot = np.stack(tabs, 1).astype(f)
    q, k = np.arange(P)[:, None], np.arange(P)[None, :]
    prev = np.where(k >= q, 0.0, MASKED)
    cur = np.where(k <= q, 0.0, MASKED)
    none = np.full((P, P), MASKED)
    masks = np.stack([np.concatenate([cur, none if w == 0 else prev], 1) for w in range(0, WINDOWS, 2)]
                     + [np.concatenate([prev, cur], 1)], 1).astype(f)
    return {"eye": eye, "rot": rot, "masks": masks}


def adaln_block(nc, x, Wq, bq, Wk, bk, Wv, bv, Wo, bo, wqkv, q_scale, k_scale, wo, ln_g, ln_b, w1, b1, w2, b2,
            c_in, wmod, eye, rot, masks, out):
    ctx = ExitStack()
    with ctx, nc.allow_non_contiguous_dma(reason="small per-feature vectors, a feature a partition"):
        def sb(name, shape, dt=F32, at=ctx):
            return at.enter_context(nc.sbuf_tensor(name, shape, dt))

        def sem(name):
            return ctx.enter_context(nc.semaphore(name))

        xT = sb("xT", [P, HALVES, N])
        identf = sb("identf", [P, P])
        ones_ln = sb("ones_ln", [P, P])
        ones = sb("ones", [P, DH])
        mod = sb("mod", [P, 12, B])
        modb = sb("modb", [P, 12])
        csil = sb("csil", [P, HALVES, B])
        gsign = sb("gsign", [P, 2, HALVES, B])
        gsize = sb("gsize", [P, 2, HALVES, B])
        bo_t = sb("bo_t", [P, HALVES])
        bo_all = sb("bo_all", [P, HALVES])
        gabo = sb("gabo", [P, HALVES])
        epst = sb("epst", [P, 1])
        minus_half = sb("minus_half", [P, 1])
        bv_t = sb("bv_t", [P, PAIRS])

        lnc = [sb(f"lnc{i}", [P, HALVES, T]) for i in range(2)]
        lns = [sb(f"lns{i}", [P, HALVES, T]) for i in range(2)]
        lnr = [sb(f"lnr{i}", [P, T]) for i in range(2)]
        tok = [sb(f"tok{i}", [P, D]) for i in range(4)]

        att = ExitStack()
        hT = sb("hT", [P, HALVES, N], at=att)
        qhh = [sb(f"qhh{s}", [P, N], F32R, at=att) for s in range(2)]
        qlm = [sb(f"qlm{s}", [DH + 1, N], F32R, at=att) for s in range(2)]
        klh = [sb(f"klh{s}", [P, N], F32R, at=att) for s in range(2)]
        kh1 = [sb(f"kh1{s}", [DH + 1, N], F32R, at=att) for s in range(2)]
        vv = [sb(f"vv{s}", [P, KT, DH], at=att) for s in range(2)]
        wqk_h = [sb(f"wqk{s}", [P, HALVES, P], at=att) for s in range(2)]
        wv_h = [sb(f"wv{s}", [P, HALVES, DH], at=att) for s in range(2)]
        bqk_h = [sb(f"bqk{s}", [P, 1], at=att) for s in range(2)]
        wo_p = sb("wo_p", [P, D], at=att)
        prob = [sb(f"prob{i}", [P, 2 * T], at=att) for i in range(PRING)]
        acc_p = [sb(f"accp{i}", [P, 2 * T], at=att) for i in range(CP)]
        acc_d = [sb(f"accd{i}", [P, 2 * T], at=att) for i in range(CP)]
        rcp = sb("rcp", [P, T], at=att)
        oT = sb("oT", [P, N], at=att)
        mx4 = sb("mx4", [P, KT, CHUNKS], at=att)
        mx1 = sb("mx1", [P, KT], at=att)
        nmx = sb("nmx", [KT, P], F32R, at=att)
        wmod_sb = hT[:, :, 0:6 * D]
        att.close()

        ffn = ExitStack()
        xf = sb("xf", [P, HALVES, N + 1], at=ffn)
        x1 = sb("x1", [P, HALVES, N + 1], at=ffn)
        wqkv_l = sb("wqkv_l", [P, HALVES, 3 * INNER], at=ffn)
        wo_l = sb("wo_l", [P, LPAIRS, D], at=ffn)
        w1_l = sb("w1_l", [P, HALVES, 2 * HID], at=ffn)
        w2_l = sb("w2_l", [P, HT, D], at=ffn)
        vec_g = sb("vec_g", [P, HALVES], at=ffn)
        vec_b = sb("vec_b", [P, HALVES], at=ffn)
        vec_b1 = sb("vec_b1", [P, 2, HT], at=ffn)
        vec_b2 = sb("vec_b2", [P, HALVES], at=ffn)
        rot_raw = sb("rot_raw", [P, WINDOWS, 4, DH], at=ffn)
        rot_l = sb("rot_l", [P, WINDOWS, 4, DH], at=ffn)
        scales = sb("scales", [P, 4, DH], at=ffn)
        mask_b = sb("mask_b", [P, WINDOWS // 2 + 1, 2 * WIN], BF16, at=ffn)
        identb = sb("identb", [P, P], BF16, at=ffn)
        q_even = sb("q_even", [P, LPAIRS, WIN], at=ffn)
        q_odd = sb("q_odd", [P, LPAIRS, WIN], at=ffn)
        both = ExitStack()
        hc = [sb(f"hc{i}", [P, HALVES, WIN], at=both) for i in range(2)]
        qk_sq = sb("qk_sq", [P, 2 * INNER], at=both)
        qk_u = sb("qk_u", [P, 2 * INNER], at=both)
        qk_w = sb("qk_w", [P, 2 * INNER], at=both)
        ssq = sb("ssq", [P, 2 * LHEADS], at=both)
        ssc = sb("ssc", [P, 2 * LHEADS], at=both)
        rnorm = sb("rnorm", [P, 2 * LHEADS], at=both)
        k_l = sb("k_l", [P, LPAIRS, 2, WIN], at=both)
        v_l = [sb(f"v_l{i}", [P, INNER], at=both) for i in range(2)]
        lp = sb("lp", [P, LHEADS, 2 * WIN], at=both)
        lpT = sb("lpT", [P, LHEADS, 2, WIN], at=both)
        lmax = sb("lmax", [P, LHEADS], at=both)
        lneg = sb("lneg", [P, LHEADS], at=both)
        lsum = sb("lsum", [P, LHEADS], at=both)
        lrcp = sb("lrcp", [P, LHEADS], at=both)
        oL = sb("oL", [P, LPAIRS, WIN], at=both)
        both.close()
        hn = [sb(f"hn{i}", [P, HALVES, T], at=ffn) for i in range(2)]
        gl = [sb(f"gl{i}", [P, T], at=ffn) for i in range(2)]
        ug = [sb(f"ug{i}", [P, T], at=ffn) for i in range(3)]
        ffn.close()

        psum = ctx.enter_context(nc.psum_tensor("psum", [P, 8, T], F32))
        QK_B, V_B, OL_B, NORM_AT = 4, 6, 7, 2
        S_BANK, O_BANK, M_BANK = 0, 4, 6

        ld = sem("ld")
        cst = sem("cst")
        su_a, su_p, su_d = sem("su_a"), sem("su_p"), sem("su_d")
        bar = sem("bar")
        bar_left = sem("bar_left")
        x_in = [sem(f"x_in{i}") for i in range(4)]
        tp_full, tp_free = sem("tp_full"), sem("tp_free")
        ln_mu, ln_c, ln_sq, ln_var, ln_sd, ln_done = (sem("ln_" + s) for s in ("mu", "c", "sq", "var", "sd", "done"))
        ln_r = sem("ln_r")
        w_in = [sem(f"w_in{s}") for s in range(2)]
        wo_in = sem("wo_in")
        pj_full, pj_hi, pj_dup, pj_dve = sem("pj_full"), sem("pj_hi"), sem("pj_dup"), sem("pj_dve")
        ring_full, ring_free = sem("ring_full"), sem("ring_free")
        s_full, exp_done, pv_done = sem("s_full"), sem("exp_done"), sem("pv_done")
        pool_sum, dve_sum = sem("pool_sum"), sem("dve_sum")
        o_free, oT_ready = sem("o_free"), sem("oT_ready")
        mx_red, mrow = sem("mx_red"), sem("mrow")
        rcp_ok = sem("rcp_ok")
        mod_ok, x_ok = sem("mod_ok"), sem("x_ok")
        ot_full, ot_tok = sem("ot_full"), sem("ot_tok")
        stored = [sem(f"stored{i}") for i in range(4)]

        mask_f_view = rot_l[:].rearrange("p w t d -> p (w t d)")[:, 0:(WINDOWS // 2 + 1) * 2 * WIN].rearrange("p (m k) -> p m k", k=2 * WIN)
        lw_in, l1_in, msk_in, msk_ok = sem("lw_in"), sem("l1_in"), sem("msk_in"), sem("msk_ok")
        rot_ok, zp_ok = sem("rot_ok"), sem("zp_ok")
        hc_ok, qk_full, vl_full, sq_done, ss_done, rn_done = (sem(n) for n in ("hc_ok", "qk_full", "vl_full", "sq_done", "ss_done", "rn_done"))
        ru_done, rot_done, qkT_full, qkT_read, vl_read, pc_done = (sem(n) for n in ("ru_done", "rot_done", "qkT_full", "qkT_read", "vl_read", "pc_done"))
        ls_full, lmx_done, lneg_done, lexp_done, lrcp_done, lp_done = (sem(n) for n in ("ls_full", "lmx_done", "lneg_done", "lexp_done", "lrcp_done", "lp_done"))
        lpT_full, lpT_read, ol_full, ol_read, lo_full, lo_read = (sem(n) for n in ("lpT_full", "lpT_read", "ol_full", "ol_read", "lo_full", "lo_read"))
        ag_full, gelu_done, ug_done, y_full, y_read = (sem(n) for n in ("ag_full", "gelu_done", "ug_done", "y_full", "y_read"))
        fin_ok = sem("fin_ok")

        block = ctx.enter_context(nc.Block())

        PH_LOAD, PH_LN1, PH_ATT, PH_LN2, PH_L0, PH_STORE, PH = 0, 1, 2, 3, 4, 8, 9

        def head_order(hh, maxima, projects):
            order = [("scores", 0)]
            for t in range(STEPS):
                if t + 1 < STEPS:
                    order.append(("scores", t + 1))
                if maxima:
                    order += [("max", 2 * t), ("max", 2 * t + 1)]
                order.append(("values", t))
                if t == KT + 3:
                    order.append(("sum", 0))
            if projects:
                order += [("proj_qk", i) for i in range(QK_ITEMS)]
            if maxima:
                order.append(("turn", 0))
            order.append(("sum", 1))
            if projects:
                order += [("proj_v", i) for i in range(V_ITEMS)]
            if hh == 1:
                order += [("out", j) for j in range(WO_ITEMS)]
            return order

        PROLOGUE = [("proj_qk", i) for i in range(QK_ITEMS)] + [("proj_v", i) for i in range(V_ITEMS)]
        MAXIMA = [("max", j) for j in range(RING_MAX)] + [("turn", 0)]
        IN_RING = ("max", "turn", "sum", "out")

        def ringed(order, r):
            rows = []
            for kind, j in order:
                rows.append((kind, j, r))
                r += kind in IN_RING
            return rows, r

        def pair_plan(last):
            plans, r = [], RING_MAX + 1
            for hh in range(2):
                rows, r = ringed(head_order(hh, not (last and hh), not last), r)
                plans.append(rows)
            assert r == RING_PAIR + (0 if last else RING_MAX + 1)
            return plans

        def head_index(b, hp, hh):
            return b * HEADS + hp * 2 + hh

        def ring_base(b, hp):
            return b * (RING_PAIR * PAIRS) + hp * RING_PAIR

        OFF_S, OFF_POOL, OFF_DVE, OFF_RING = STEPS, CP * POOL_OPS, CP * DVE_OPS, RING_PAIR

        PLAN = {last: pair_plan(last) for last in (False, True)}

        def turn_place(last, hh):
            return [r for kind, _, r in PLAN[last][hh] if kind == "turn"][0]

        def phase_end(eng, b, phase):
            eng.drain().then_inc(bar, 1)
            eng.wait_ge(bar, b * (5 * PH) + 5 * (phase + 1))
            eng.sem_inc(bar_left, 1)

        LW_L = 16 * 9
        LW_B = LW_L * (1 + LAYERS)
        LN_B = CHUNKS * (2 + LAYERS)

        def ln_mean(pe, n, src):
            pe.wait_ge(ln_c, n + 1)
            for h in range(HALVES):
                mm = pe.matmul(psum[:, 0, :], ones_ln[:], src(h), start=(h == 0), stop=(h == HALVES - 1))
            mm.then_inc(ln_mu, 1)

        def ln_variance(pe, n, par):
            pe.wait_ge(ln_sq, n + 1)
            pe.wait_ge(ln_sd, n + 1)
            for h in range(HALVES):
                mm = pe.matmul(psum[:, 1, :], ones_ln[:], lns[par][:, h, :], start=(h == 0), stop=(h == HALVES - 1))
            mm.then_inc(ln_var, 1)

        def ln_square(act, n, par):
            act.wait_ge(ln_c, n + 2)
            act.wait_ge(ln_var, n + 1)
            act.activation(lns[par][:], lnc[par][:], ACT.Square).then_inc(ln_sq, 1)

        def ln_deviation(act, n, par):
            act.wait_ge(ln_var, n + 3)
            act.wait_ge(ln_done, n + 1)
            act.activation(lnr[par][:], psum[:, 1, :], ACT.Sqrt, bias=epst[:, 0:1]).then_inc(ln_sd, 1)

        def ln_centre(dve, n, par, src):
            dve.wait_ge(ln_mu, n + 1)
            dve.wait_ge(ln_done, n + 1)
            for h in range(HALVES):
                op = dve.tensor_tensor(lnc[par][:, h, :], src(h), psum[:, 0, :], ALU.subtract)
            op.then_inc(ln_c, 1)

        def ln_scale(dve, n, par, dst, gain, shift):
            dve.wait_ge(ln_sd, n + 2)
            dve.wait_ge(ln_sq, n + 1)
            dve.reciprocal(lnr[par][:], lnr[par][:]).then_inc(ln_r, 1)
            dve.wait_ge(ln_r, n * 3 + 1)
            for h in range(HALVES):
                dve.scalar_tensor_tensor(lnc[par][:, h, :], lnc[par][:, h, :], gain(h), lnr[par][:],
                                         ALU.mult, ALU.mult).then_inc(ln_r, 1)
            dve.wait_ge(ln_r, n * 3 + 3)
            for h in range(HALVES):
                op = dve.tensor_scalar(dst(h), lnc[par][:, h, :], shift(h), None, ALU.add)
            op.then_inc(ln_done, 1)

        def xt(c):
            return lambda h: xT[:, h, c * T:(c + 1) * T]

        def ln_pe(pe, n0):
            ln_mean(pe, n0, xt(0))
            for c in range(CHUNKS):
                if c + 1 < CHUNKS:
                    ln_mean(pe, n0 + c + 1, xt(c + 1))
                ln_variance(pe, n0 + c, c % 2)

        def ln_act(act, n0):
            ln_square(act, n0, 0)
            for c in range(CHUNKS):
                if c + 1 < CHUNKS:
                    ln_square(act, n0 + c + 1, (c + 1) % 2)
                ln_deviation(act, n0 + c, c % 2)

        def ln_dve(dve, n0, dst, gain, shift):
            ln_centre(dve, n0, 0, xt(0))
            for c in range(CHUNKS):
                if c + 1 < CHUNKS:
                    ln_centre(dve, n0 + c + 1, (c + 1) % 2, xt(c + 1))
                ln_scale(dve, n0 + c, c % 2, dst(c), gain, shift)

        def layer_index(b, l):
            return b * LAYERS + l

        def columns(t0, size, shifted=0):
            start = t0 + (1 - shifted)
            return slice(start, start + size) if isinstance(start, int) else bass.ds(start, size)

        def windows(eng, prologue, body):
            prologue()
            with eng.Fori(0, WINDOWS // 2 - 1) as i:
                for par in range(2):
                    body(i, par, True)
            for par in range(2):
                body(WINDOWS // 2 - 1, par, par == 0)

        def mlp(eng, prologue, chunk):
            prologue()
            with eng.Fori(0, CHUNKS // 2 - 1) as i:
                for par in range(2):
                    chunk(i, par, True)
            for par in range(2):
                chunk(CHUNKS // 2 - 1, par, par == 0)

        @block.sync
        def _(sp):
            for dst, src in ((identf[:], eye), (bo_t[:], bo.rearrange("(m p) -> p m", p=P)),
                             (bv_t[:], bv.rearrange("(m p) -> p m", p=P)),
                             (csil[:, 0, :], c_in[:, 0:P].rearrange("b p -> p b")),
                             (csil[:, 1, :], c_in[:, P:D].rearrange("b p -> p b")),
                             (wmod_sb, wmod.rearrange("(h p) n -> p h n", p=P)),
                             ):
                sp.dma_start(dst, src).then_inc(ld, 16)
            sp.dma_start(prob[0][:].rearrange("p (m n) -> p m n", n=D), Wo[0:4 * P, :].rearrange("(m p) n -> p m n", p=P)).then_inc(ld, 16)
            sp.dma_start(prob[1][:].rearrange("p (m n) -> p m n", n=D), Wo[4 * P:8 * P, :].rearrange("(m p) n -> p m n", p=P)).then_inc(ld, 16)
            sp.wait_ge(su_d, 8)
            sp.sem_inc(mrow, 16)
            with sp.Fori(0, B) as b:
                for t in range(KT):
                    if t >= 4:
                        sp.wait_ge(tp_full, b * KT + (t - 4) + 1)
                    sp.dma_start(tok[t % 4][:], x[bass.ds(b, 1), t * P:(t + 1) * P, :].rearrange("o p d -> (o p) d")).then_inc(x_in[t % 4], 16)
                phase_end(sp, b, PH_LOAD)
                phase_end(sp, b, PH_LN1)

                def load_head(hexpr, s):
                    cols = slice(hexpr * DH, hexpr * DH + DH) if isinstance(hexpr, int) else bass.ds(hexpr * DH, DH)
                    for w, lo in ((Wq, 0), (Wk, DH)):
                        sp.dma_start(wqk_h[s][:, :, lo:lo + DH], w[:, cols].rearrange("(h p) n -> p h n", p=P)).then_inc(w_in[s], 16)
                    sp.dma_start(wv_h[s][:], Wv[:, cols].rearrange("(h p) n -> p h n", p=P)).then_inc(w_in[s], 16)
                    sp.dma_start(bqk_h[s][0:DH, :], bq[cols].rearrange("(p o) -> p o", o=1)).then_inc(w_in[s], 16)
                    sp.dma_start(bqk_h[s][DH:P, :], bk[cols].rearrange("(p o) -> p o", o=1)).then_inc(w_in[s], 16)

                def load_wo(b, hp):
                    sp.wait_ge(ring_full, OFF_RING + ring_base(b, hp) + RING_MAX + 1)
                    sp.dma_start(wo_p[:], Wo[bass.ds(hp * P, P), :]).then_inc(wo_in, 16)

                def store_max(b, hp, place, s):
                    sp.wait_ge(ring_free, OFF_RING + 2 + ring_base(b, hp) + place + 1)
                    sp.dma_start(qlm[s][DH:DH + 1, :].bitcast(F32).rearrange("o (t p) -> o t p", p=P),
                                 nmx[:].bitcast(F32)).then_inc(mrow, 16)

                def free_head(b, hp, hh):
                    sp.wait_ge(pj_dup, head_index(b, hp, hh) * QK_ITEMS + QK_ITEMS)
                    sp.wait_ge(pj_dve, head_index(b, hp, hh) * PJ_ITEMS + PJ_ITEMS)
                load_head(0, 0)
                load_head(1, 1)
                store_max(b, 0, RING_MAX, 0)
                with sp.Fori(0, PAIRS - 1) as hp:
                    load_wo(b, hp)
                    free_head(b, hp, 0)
                    load_head(hp * 2 + 2, 0)
                    store_max(b, hp, turn_place(False, 0), 1)
                    free_head(b, hp, 1)
                    load_head(hp * 2 + 3, 1)
                    store_max(b, hp, turn_place(False, 1), 0)
                load_wo(b, PAIRS - 1)
                store_max(b, PAIRS - 1, turn_place(True, 0), 1)
                sp.wait_ge(mrow, b * (16 * HEADS) + 16 + 16 * HEADS)
                sp.sem_inc(bar_left, 1)
                phase_end(sp, b, PH_ATT)
                for dst, src in ((rot_raw[:], rot.rearrange("(w p) t d -> p w t d", p=P)), (mask_f_view, masks)):
                    sp.dma_start(dst, src).then_inc(msk_in, 16)

                def load_attention(l):
                    at_l = slice(l, l + 1) if isinstance(l, int) else bass.ds(l, 1)
                    for h in range(HALVES):
                        sp.dma_start(wqkv_l[:, h, :], wqkv[at_l, h * P:(h + 1) * P, :].rearrange("o p n -> (o p) n")).then_inc(lw_in, 16)
                    sp.dma_start(wo_l[:], wo[at_l].rearrange("o (k p) n -> p (o k) n", p=P)).then_inc(lw_in, 16)
                    for j, v in ((0, q_scale), (2, k_scale)):
                        row = v[at_l, :]
                        sp.dma_start(scales[:, j, :], row.broadcast_to([P, DH])).then_inc(lw_in, 16)
                        for o in range(2):
                            sp.dma_start(scales[:, j + 1, o * 32:(o + 1) * 32], row[:, (1 - o) * 32:(2 - o) * 32].broadcast_to([P, 32])).then_inc(lw_in, 16)

                def load_mlp(l):
                    at_l = bass.ds(l, 1)
                    for h in range(HALVES):
                        sp.dma_start(w1_l[:, h, :], w1[at_l, h * P:(h + 1) * P, :].rearrange("o p n -> (o p) n")).then_inc(l1_in, 16)
                    full = (HT - 1) * P
                    sp.dma_start(w2_l[:, 0:HT - 1, :], w2[at_l, 0:full, :].rearrange("o (k p) n -> p (o k) n", p=P)).then_inc(l1_in, 16)
                    sp.dma_start(w2_l[0:HID - full, HT - 1, :], w2[at_l, full:HID, :].rearrange("o p n -> (o p) n")).then_inc(l1_in, 16)
                    for dst, src in ((vec_g, ln_g), (vec_b, ln_b), (vec_b2, b2)):
                        sp.dma_start(dst[:], src[at_l, :].rearrange("o (h p) -> p (o h)", p=P)).then_inc(l1_in, 16)
                    for j in range(2):
                        sp.dma_start(vec_b1[:, j, 0:HT - 1], b1[at_l, j * HID:j * HID + full].rearrange("o (k p) -> p (o k)", p=P)).then_inc(l1_in, 16)
                        sp.dma_start(vec_b1[0:HID - full, j, HT - 1:HT], b1[at_l, j * HID + full:(j + 1) * HID].rearrange("o p -> p o")).then_inc(l1_in, 16)
                load_attention(0)
                phase_end(sp, b, PH_LN2)
                with sp.Fori(0, LAYERS) as l:
                    load_mlp(l)
                    phase_end(sp, b, PH_L0 + l * 2)
                    load_attention(LAYERS - 1)
                    phase_end(sp, b, PH_L0 + l * 2 + 1)
                for t in range(KT):
                    sp.wait_ge(ot_tok, b * KT + t + 1)
                    sp.dma_start(out[bass.ds(b, 1), t * P:(t + 1) * P, :].rearrange("o p d -> (o p) d"), tok[t % 4][:]).then_inc(stored[t % 4], 16)
                for i in range(4):
                    sp.wait_ge(stored[i], b * (4 * KT) + 4 * KT)
                sp.sem_inc(bar_left, 1)
                phase_end(sp, b, PH_STORE)

        @block.gpsimd
        def _(pool):
            pool.memset(ones_ln[:], 1.0 / D)
            pool.memset(ones[:], 1.0)
            pool.memset(epst[:], EPS).then_inc(cst, 1)
            pool.wait_ge(cst, 1)
            pool.memset(minus_half[:], -0.5).then_inc(cst, 1)
            pool.wait_ge(cst, 2)
            pool.sem_inc(pool_sum, OFF_POOL)
            with pool.Fori(0, B) as b:
                phase_end(pool, b, PH_LOAD)
                phase_end(pool, b, PH_LN1)

                def head_sums(G):
                    for cp in range(CP):
                        for i in range(1, len(SUM_POOL)):
                            kt = SUM_POOL[i]
                            pool.wait_ge(exp_done, G * STEPS + cp * KT + kt + 1)
                            n = G * (CP * POOL_OPS) + OFF_POOL + cp * POOL_OPS + i - 1
                            pool.wait_ge(pool_sum, n)
                            first = prob[SUM_POOL[0] % PRING] if i == 1 else acc_p[cp]
                            pool.tensor_tensor(acc_p[cp][:], first[:], prob[kt % PRING][:], ALU.add).then_inc(pool_sum, 1)

                with pool.Fori(0, PAIRS) as hp:
                    for hh in range(2):
                        head_sums(head_index(b, hp, hh))
                phase_end(pool, b, PH_ATT)
                phase_end(pool, b, PH_LN2)
                with pool.Fori(0, LAYERS) as l:
                    n0 = layer_index(b, l) * WINDOWS

                    def inverse_norm(n):
                        pool.wait_ge(ss_done, n * 2 + 2)
                        pool.tensor_tensor(rnorm[:], ssc[:], minus_half[:, 0:1].broadcast_to([P, 2 * LHEADS]), ALU.pow).then_inc(rn_done, 1)

                    def scale_probs(n, it):
                        pool.wait_ge(lrcp_done, n * ITEMS + it + 1)
                        hs = slice(it * IH, (it + 1) * IH)
                        pool.tensor_tensor(lp[:, hs, :], lp[:, hs, :], lrcp[:, hs].unsqueeze(2).broadcast_to([P, IH, 2 * WIN]), ALU.mult).then_inc(lp_done, 1)

                    def pool_window(i, par, has_next):
                        n = n0 + i * 2 + par
                        scale_probs(n, 0)
                        scale_probs(n, 1)
                        if has_next:
                            inverse_norm(n + 1)
                    windows(pool, lambda: inverse_norm(n0), pool_window)
                    phase_end(pool, b, PH_L0 + l * 2)
                    phase_end(pool, b, PH_L0 + l * 2 + 1)
                phase_end(pool, b, PH_STORE)

        @block.scalar
        def _(act):
            act.wait_ge(ld, 16 * 8)
            act.activation(csil[:], csil[:], ACT.Silu).then_inc(su_a, 1)
            for s, n in ((ln_sd, 1), (qkT_read, 1), (vl_read, 1), (lpT_read, ITEMS)):
                act.sem_inc(s, n)
            with act.Fori(0, B) as b:
                for t in range(KT):
                    act.wait_ge(tp_full, b * KT + t + 1)
                    act.activation(xT[:, :, t * P:(t + 1) * P], psum[:, t % 4, 0:D].rearrange("p (h n) -> p h n", h=HALVES),
                                   ACT.Copy).then_inc(tp_free, 1)
                phase_end(act, b, PH_LOAD)
                ln_act(act, b * LN_B)
                phase_end(act, b, PH_LN1)

                def project(G, s):
                    for i in range(QK_ITEMS):
                        cols = slice(i * T, (i + 1) * T)
                        ps = psum[:, S_BANK + i % 4, :]
                        act.wait_ge(pj_full, G * PJ_ITEMS + i + 1)
                        act.activation(qhh[s][0:DH, cols], ps[0:DH], ACT.Identity, bias=bqk_h[s][0:DH, 0:1])
                        act.activation(klh[s][DH:P, cols], ps[DH:P], ACT.Identity, bias=bqk_h[s][DH:P, 0:1]).then_inc(pj_hi, 1)
                        act.wait_ge(pj_hi, G * QK_ITEMS + i + 1)
                        act.activation(qhh[s][DH:P, cols], qhh[s][0:DH, cols], ACT.Copy).then_inc(pj_dup, 1)

                def exps(G):
                    for t in range(STEPS):
                        act.wait_ge(s_full, G * STEPS + t + 1)
                        act.wait_ge(pv_done, G * STEPS + OFF_S + t - PRING + 1)
                        cp, kt = divmod(t - PRING, KT)
                        if kt in SUM_DVE:
                            act.wait_ge(dve_sum, G * (CP * DVE_OPS) + OFF_DVE + cp * DVE_OPS + SUM_DVE.index(kt) + 1)
                        else:
                            act.wait_ge(pool_sum, G * (CP * POOL_OPS) + OFF_POOL + cp * POOL_OPS + max(SUM_POOL.index(kt), 1))
                        act.activation(prob[t % PRING][:], psum[:, S_BANK + 2 * (t % 2):S_BANK + 2 * (t % 2) + 2, :].rearrange("p a b -> p (a b)"),
                                       ACT.Exp, scale=float(ATT_SCALE)).then_inc(exp_done, 1)
                project(head_index(b, 0, 0), 0)
                project(head_index(b, 0, 1), 1)
                with act.Fori(0, PAIRS - 1) as hp:
                    for hh in range(2):
                        exps(head_index(b, hp, hh))
                        project(head_index(b, hp + 1, hh), hh)
                for hh in range(2):
                    exps(head_index(b, PAIRS - 1, hh))
                phase_end(act, b, PH_ATT)
                ln_act(act, b * LN_B + CHUNKS)
                phase_end(act, b, PH_LN2)
                with act.Fori(0, LAYERS) as l:
                    n0 = layer_index(b, l) * WINDOWS

                    def square(n):
                        act.wait_ge(qk_full, n + 1)
                        act.activation(qk_sq[:], psum[:, QK_B:QK_B + 2, :].rearrange("p a n -> p (a n)"), ACT.Square).then_inc(sq_done, 1)

                    def read_turned(n, par):
                        act.wait_ge(qkT_full, n + 1)
                        qT = psum[:, QK_B, :].rearrange("p (m n) -> p m n", n=WIN)
                        act.activation(q_even[0:DH], qT[0:DH], ACT.Copy)
                        act.activation(q_odd[DH:P], qT[DH:P], ACT.Copy)
                        act.activation(k_l[:, :, par, :], psum[:, QK_B + 1, :].rearrange("p (m n) -> p m n", n=WIN), ACT.Copy).then_inc(qkT_read, 1)

                    def read_values(n, par):
                        act.wait_ge(vl_full, n + 1)
                        act.activation(v_l[par][:], psum[:, V_B, :], ACT.Copy).then_inc(vl_read, 1)

                    def exp_item(n, it):
                        act.wait_ge(lneg_done, n * ITEMS + it + 1)
                        for h in range(IH):
                            hh = it * IH + h
                            op = act.activation(lp[:, hh, :], psum[:, 2 * it + h // 2, (h % 2) * 2 * WIN:(h % 2 + 1) * 2 * WIN], ACT.Exp,
                                                bias=lneg[:, hh:hh + 1], scale=QK_SCALE, accum_out=lsum[:, hh:hh + 1])
                        op.then_inc(lexp_done, 1)

                    def read_probs(n, it):
                        act.wait_ge(lpT_full, n * ITEMS + it + 1)
                        act.activation(lpT[:, it * IH:(it + 1) * IH].rearrange("p h s n -> p (h s n)"),
                                       psum[:, 2 * it:2 * it + 2, :].rearrange("p a n -> p (a n)"), ACT.Copy).then_inc(lpT_read, 1)

                    def act_prologue():
                        square(n0)
                        read_values(n0, 0)
                        read_turned(n0, 0)

                    def act_window(i, par, has_next):
                        n = n0 + i * 2 + par
                        exp_item(n, 0)
                        exp_item(n, 1)
                        if has_next:
                            square(n + 1)
                        read_probs(n, 0)
                        read_probs(n, 1)
                        act.wait_ge(ol_full, n + 1)
                        act.activation(oL[:].rearrange("p m n -> p (m n)"), psum[:, OL_B, :], ACT.Copy).then_inc(ol_read, 1)
                        if has_next:
                            read_values(n + 1, 1 - par)
                            read_turned(n + 1, 1 - par)
                    windows(act, act_prologue, act_window)
                    phase_end(act, b, PH_L0 + l * 2)

                    m0, q0 = layer_index(b, l) * CHUNKS, b * LN_B + 2 * CHUNKS + l * CHUNKS
                    act.wait_ge(l1_in, (layer_index(b, l) + 1) * (16 * 11))

                    def act_norm(c, par):
                        ln_square(act, q0 + c, par)
                        ln_deviation(act, q0 + c, par)

                    def act_chunk(i, par, has_next):
                        for t, (o, size) in enumerate(HID_TILES):
                            k = (m0 + i * 2 + par) * HT + t
                            act.wait_ge(ag_full, k + 1)
                            act.wait_ge(ug_done, k + 1)
                            act.activation(gl[t % 2][0:size, :], psum[0:size, 4 + t % 2, :], ACT.Gelu, bias=vec_b1[0:size, 1, t:t + 1]).then_inc(gelu_done, 1)
                            if has_next and t == NORM_AT:
                                ln_square(act, q0 + i * 2 + par + 1, 1 - par)
                        if has_next:
                            ln_deviation(act, q0 + i * 2 + par + 1, 1 - par)
                    mlp(act, lambda: act_norm(0, 0), act_chunk)
                    phase_end(act, b, PH_L0 + l * 2 + 1)
                phase_end(act, b, PH_STORE)

        @block.vector
        def _(dve):
            dve.wait_ge(su_p, 1)
            dve.tensor_copy(mod[:], psum[:, 0, 0:12 * B].rearrange("p (j b) -> p j b", b=B)).then_inc(su_d, 1)
            dve.wait_ge(su_d, 1)
            for j0 in (2, 8):
                dve.tensor_scalar(mod[:, j0:j0 + 2, :], mod[:, j0:j0 + 2, :], 1.0, None, ALU.add).then_inc(su_d, 1)
            dve.wait_ge(ld, 16 * 8)
            dve.tensor_tensor(bo_all[:], psum[:, 1, 0:HALVES], bo_t[:], ALU.add).then_inc(su_d, 1)
            gview = mod[:].rearrange("p (g k) b -> p g k b", g=2)[:, :, 4:6, :]
            dve.tensor_scalar(gsign[:], gview, 0.0, 2.0, ALU.is_ge, ALU.mult).then_inc(su_d, 1)
            dve.scalar_tensor_tensor(gsize[:], gview, -1.0, gview, ALU.mult, ALU.max).then_inc(su_d, 1)
            dve.wait_ge(su_d, 6)
            dve.tensor_scalar(gsize[:], gsize[:], 0.25, None, ALU.max).then_inc(su_d, 1)
            dve.wait_ge(su_d, 7)
            dve.scalar_tensor_tensor(gview, gsign[:], -1.0, gsize[:], ALU.add, ALU.mult).then_inc(su_d, 1)
            dve.wait_ge(su_d, 8)
            for s, n in ((ring_free, OFF_RING + 2), (dve_sum, OFF_DVE), (o_free, CP),
                         (ln_c, 1), (ln_done, 2), (ug_done, 2), (y_read, 1), (lo_read, 1)):
                dve.sem_inc(s, n)
            with dve.Fori(0, B) as b:
                phase_end(dve, b, PH_LOAD)
                for s in range(2):
                    dve.memset(kh1[s][DH:DH + 1, :].bitcast(F32), 1.0)
                dve.tensor_copy(modb[:], mod[:, :, bass.ds(b, 1)].rearrange("p j o -> p (j o)")).then_inc(mod_ok, 1)
                dve.wait_ge(mod_ok, b * 2 + 1)
                dve.tensor_tensor(gabo[:], modb[:, 4:6], bo_all[:], ALU.mult).then_inc(mod_ok, 1)
                dve.wait_ge(mod_ok, b * 2 + 2)
                ln_dve(dve, b * LN_B, lambda c: lambda h: hT[:, h, c * T:(c + 1) * T],
                       lambda h: modb[:, 2 + h:3 + h], lambda h: modb[:, h:h + 1])
                for h in range(HALVES):
                    dve.tensor_scalar(xT[:, h, :], xT[:, h, :], gabo[:, h:h + 1], None, ALU.add)
                phase_end(dve, b, PH_LN1)

                def proj_qk(G, s, i):
                    cols = slice(i * T, (i + 1) * T)
                    ps = psum[:, S_BANK + i % 4, :]
                    dve.wait_ge(pj_hi, G * QK_ITEMS + i + 1)
                    dve.tensor_copy(kh1[s][0:DH, cols], klh[s][DH:P, cols])
                    dve.scalar_tensor_tensor(qlm[s][0:DH, cols], ps[0:DH], bqk_h[s][0:DH, 0:1], qhh[s][0:DH, cols], ALU.add, ALU.subtract)
                    dve.scalar_tensor_tensor(klh[s][0:DH, cols], ps[DH:P], bqk_h[s][DH:P, 0:1], klh[s][DH:P, cols], ALU.add, ALU.subtract).then_inc(pj_dve, 1)

                def proj_v(G, s, i):
                    dve.wait_ge(pj_full, G * PJ_ITEMS + QK_ITEMS + i + 1)
                    dve.tensor_copy(vv[s][:, i * 8:(i + 1) * 8, :], psum[:, S_BANK + i, :].rearrange("p (t d) -> p t d", d=DH)).then_inc(pj_dve, 1)

                def ring_wait(rb, i):
                    dve.wait_ge(ring_full, OFF_RING + rb + i + 1)
                    return psum[:, M_BANK + i % 2, :]

                def max_tile(rb, i, j):
                    ps = ring_wait(rb, i)
                    dve.tensor_reduce(mx4[:, j // CHUNKS, j % CHUNKS:j % CHUNKS + 1], ps, AX_X, ALU.max).then_inc(ring_free, 1)

                def max_all(rb, r):
                    dve.wait_ge(ring_free, OFF_RING + 2 + rb + r)
                    dve.tensor_reduce(mx1[:], mx4[:], AX_X, ALU.max).then_inc(mx_red, 1)

                def max_neg(G, rb, r):
                    ps = ring_wait(rb, r)
                    dve.wait_ge(mrow, G * 16 + 16)
                    dve.tensor_scalar(nmx[:], ps[0:KT, 0:P], -1.0, None, ALU.mult).then_inc(ring_free, 1)

                def add_sum(G, cp, j):
                    kt = SUM_DVE[j]
                    dve.wait_ge(exp_done, G * STEPS + cp * KT + kt + 1)
                    if j:
                        dve.wait_ge(dve_sum, G * (CP * DVE_OPS) + OFF_DVE + cp * DVE_OPS + j)
                        dve.tensor_tensor(acc_d[cp][:], acc_d[cp][:], prob[kt % PRING][:], ALU.add).then_inc(dve_sum, 1)
                    else:
                        dve.tensor_copy(acc_d[cp][:], prob[kt % PRING][:]).then_inc(dve_sum, 1)

                def normalise(G, rb, i, hh, cp):
                    ps = ring_wait(rb, i)
                    dve.reciprocal(rcp[:], ps).then_inc(ring_free, 1)
                    dve.wait_ge(ring_free, OFF_RING + 2 + rb + i + 1)
                    dve.wait_ge(pv_done, G * STEPS + OFF_S + (cp + 1) * KT)
                    for j in range(2):
                        rows = slice(j * DH, (j + 1) * DH)
                        op = dve.tensor_tensor(oT[hh * DH:(hh + 1) * DH, (2 * cp + j) * T:(2 * cp + j + 1) * T],
                                               psum[rows, O_BANK + cp, :], rcp[rows, :], ALU.mult)
                    op.then_inc(o_free, 1)

                def out_tile(rb, i, j):
                    ps = ring_wait(rb, i)
                    c, m = divmod(j, HALVES)
                    xs = xT[:, m, c * T:(c + 1) * T]
                    dve.scalar_tensor_tensor(xs, ps, modb[:, 4 + m:5 + m], xs, ALU.mult, ALU.add).then_inc(ring_free, 1)

                def head(b, hp, hh, plan):
                    G, rb, s = head_index(b, hp, hh), ring_base(b, hp), hh
                    for kind, j, r in plan:
                        if kind == "max":
                            max_tile(rb, r, j)
                            if j == RING_MAX - 1:
                                max_all(rb, r + 1 + (RING_MAX - 1 - j))
                        elif kind == "turn":
                            max_neg(G + 1, rb, r)
                        elif kind == "values":
                            cp, kt = divmod(j, KT)
                            if kt in SUM_DVE:
                                add_sum(G, cp, SUM_DVE.index(kt))
                        elif kind == "sum":
                            normalise(G, rb, r, hh, j)
                        elif kind == "proj_qk":
                            proj_qk(G + 2, s, j)
                        elif kind == "proj_v":
                            proj_v(G + 2, s, j)
                        elif kind == "out":
                            out_tile(rb, r, j)
                for hh in range(2):
                    for kind, j in PROLOGUE:
                        (proj_qk if kind == "proj_qk" else proj_v)(head_index(b, 0, hh), hh, j)
                for j in range(RING_MAX):
                    max_tile(ring_base(b, 0), j, j)
                max_all(ring_base(b, 0), RING_MAX)
                max_neg(head_index(b, 0, 0), ring_base(b, 0), RING_MAX)
                with dve.Fori(0, PAIRS - 1) as hp:
                    for hh in range(2):
                        head(b, hp, hh, PLAN[False][hh])
                for hh in range(2):
                    head(b, PAIRS - 1, hh, PLAN[True][hh])
                phase_end(dve, b, PH_ATT)
                for z in (xf[:, :, 0:1], x1[:, :, 0:1], q_even[DH:P], q_odd[0:DH]):
                    dve.memset(z, 0.0)
                dve.wait_ge(msk_in, b * 32 + 32)
                dve.tensor_copy(mask_b[:], mask_f_view)
                dve.tensor_copy(identb[:], identf[:]).then_inc(msk_ok, 1)
                ln_dve(dve, b * LN_B + CHUNKS, lambda c: lambda h: xf[:, h, columns(c * T, T)],
                       lambda h: modb[:, 8 + h:9 + h], lambda h: modb[:, 6 + h:7 + h])
                phase_end(dve, b, PH_LN2)
                with dve.Fori(0, LAYERS) as l:
                    n0 = layer_index(b, l) * WINDOWS
                    dve.memset(k_l[:, :, 1, :], 0.0)
                    dve.memset(v_l[1][:], 0.0).then_inc(zp_ok, 1)

                    def window_input(n, w, par):
                        for h in range(HALVES):
                            op = dve.tensor_scalar(hc[par][:, h, :], xf[:, h, columns(w * WIN, WIN, shifted=h)], 1.0, None, ALU.mult)
                        op.then_inc(hc_ok, 1)

                    def rotate(n, w):
                        dve.wait_ge(sq_done, n + 1)
                        dve.tensor_reduce(ssq[:], qk_sq[:].rearrange("p (h d) -> p h d", d=DH), AX_X, ALU.add).then_inc(ss_done, 1)
                        dve.wait_ge(ss_done, n * 2 + 1)
                        dve.tensor_scalar(ssc[:], ssq[:], 1e-24, None, ALU.max).then_inc(ss_done, 1)
                        at = bass.ds(w, 1) if not isinstance(w, int) else slice(w, w + 1)
                        qk = psum[:, QK_B:QK_B + 2, :].rearrange("p a (h d) -> p a h d", d=DH)
                        u = qk_u[:].rearrange("p (a h d) -> p a h d", a=2, d=DH)
                        v = qk_w[:].rearrange("p (a h d) -> p a h d", a=2, d=DH)
                        tab = rot_l[:, at].rearrange("p o (a t) d -> p (o a) t d", a=2)
                        for a in range(2):
                            dve.tensor_tensor(u[:, a], qk[:, a], tab[:, a, 0:1, :].broadcast_to([P, LHEADS, DH]), ALU.mult)
                            for o in range(2):
                                dst, src = slice(o * 32, (o + 1) * 32), slice((1 - o) * 32, (2 - o) * 32)
                                op = dve.tensor_tensor(v[:, a, :, dst], qk[:, a, :, src],
                                                       tab[:, a, 1:2, dst].broadcast_to([P, LHEADS, 32]), ALU.mult)
                        op.then_inc(ru_done, 1)
                        dve.wait_ge(ru_done, n * 2 + 1)
                        dve.tensor_tensor(qk_u[:], qk_u[:], qk_w[:], ALU.add).then_inc(ru_done, 1)
                        dve.wait_ge(ru_done, n * 2 + 2)
                        dve.wait_ge(rn_done, n + 1)
                        dve.tensor_tensor(qk_w[:].rearrange("p (h d) -> p h d", d=DH), qk_u[:].rearrange("p (h d) -> p h d", d=DH),
                                          rnorm[:].unsqueeze(2).broadcast_to([P, 2 * LHEADS, DH]), ALU.mult).then_inc(rot_done, 1)

                    def item_max(n, it):
                        hs = slice(it * IH, (it + 1) * IH)
                        dve.wait_ge(ls_full, n * ITEMS + it + 1)
                        dve.tensor_reduce(lmax[:, hs], psum[:, 2 * it:2 * it + 2, :].rearrange("p a (h k) -> p (a h) k", k=2 * WIN), AX_X, ALU.max).then_inc(lmx_done, 1)
                        dve.wait_ge(lmx_done, n * ITEMS + it + 1)
                        dve.tensor_scalar(lneg[:, hs], lmax[:, hs], -QK_SCALE, None, ALU.mult).then_inc(lneg_done, 1)

                    def item_rcp(n, it):
                        hs = slice(it * IH, (it + 1) * IH)
                        dve.wait_ge(lexp_done, n * ITEMS + it + 1)
                        dve.reciprocal(lrcp[:, hs], lsum[:, hs]).then_inc(lrcp_done, 1)

                    def dve_prologue():
                        dve.wait_ge(lw_in, b * LW_B + (l + 1) * LW_L)
                        dve.tensor_tensor(rot_l[:].rearrange("p w t d -> p w (t d)"), rot_raw[:].rearrange("p w t d -> p w (t d)"),
                                          scales[:].rearrange("p t d -> p (t d)").unsqueeze(1).broadcast_to([P, WINDOWS, 4 * DH]), ALU.mult).then_inc(rot_ok, 1)
                        dve.wait_ge(rot_ok, layer_index(b, l) + 1)
                        window_input(n0, 0, 0)
                        rotate(n0, 0)

                    def dve_window(i, par, has_next):
                        w = i * 2 + par
                        n = n0 + w
                        if has_next:
                            window_input(n + 1, w + 1, 1 - par)
                        item_max(n, 0)
                        item_max(n, 1)
                        item_rcp(n, 0)
                        item_rcp(n, 1)
                        if has_next:
                            rotate(n + 1, w + 1)
                        dve.wait_ge(lo_full, n + 1)
                        cols = columns(w * WIN, WIN)
                        dve.tensor_tensor(x1[:, :, cols], xf[:, :, cols], psum[:, OL_B, 0:HALVES * WIN].rearrange("p (h n) -> p h n", n=WIN), ALU.add).then_inc(lo_read, 1)
                    windows(dve, dve_prologue, dve_window)
                    phase_end(dve, b, PH_L0 + l * 2)

                    m0, q0 = layer_index(b, l) * CHUNKS, b * LN_B + 2 * CHUNKS + l * CHUNKS
                    dve.wait_ge(l1_in, (layer_index(b, l) + 1) * (16 * 11))

                    def gain(h):
                        return vec_g[:, h:h + 1]

                    def shift(h):
                        return vec_b[:, h:h + 1]

                    def shifted_src(c):
                        return lambda h: x1[:, h, columns(c * T, T, shifted=h)]

                    def dve_mlp_prologue():
                        ln_centre(dve, q0, 0, shifted_src(0))
                        ln_scale(dve, q0, 0, lambda h: hn[0][:, h, :], gain, shift)

                    def dve_chunk(i, par, has_next):
                        c = i * 2 + par
                        m = m0 + c
                        for t, (o, size) in enumerate(HID_TILES):
                            k = m * HT + t
                            if has_next and t == NORM_AT:
                                ln_centre(dve, q0 + c + 1, 1 - par, shifted_src(c + 1))
                            dve.wait_ge(gelu_done, k + 1)
                            dve.scalar_tensor_tensor(ug[t % 3][0:size, :], psum[0:size, 2 + t % 2, :], vec_b1[0:size, 0, t:t + 1], gl[t % 2][0:size, :],
                                                     ALU.add, ALU.mult).then_inc(ug_done, 1)
                        if has_next:
                            ln_scale(dve, q0 + c + 1, 1 - par, lambda h: hn[1 - par][:, h, :], gain, shift)
                        dve.wait_ge(y_full, m + 1)
                        for h in range(HALVES):
                            op = dve.scalar_tensor_tensor(xf[:, h, columns(c * T, T)], psum[:, 6 + h, :], vec_b2[:, h:h + 1], x1[:, h, columns(c * T, T)], ALU.add, ALU.add)
                        op.then_inc(y_read, 1)
                    mlp(dve, dve_mlp_prologue, dve_chunk)
                    phase_end(dve, b, PH_L0 + l * 2 + 1)
                for h in range(HALVES):
                    op = dve.scalar_tensor_tensor(xT[:, h, :], xf[:, h, 1:N + 1], modb[:, 10 + h:11 + h], xT[:, h, :], ALU.mult, ALU.add)
                op.then_inc(fin_ok, 1)
                for t in range(KT):
                    dve.wait_ge(ot_full, b * KT + t + 1)
                    if t >= 4:
                        dve.wait_ge(stored[t % 4], b * (4 * KT) + 16 * (t // 4))
                    dve.tensor_copy(tok[t % 4][:], psum[:, t % 4, 0:D]).then_inc(ot_tok, 1)
                phase_end(dve, b, PH_STORE)

        @block.tensor
        def _(pe):
            pe.wait_ge(su_a, 1)
            pe.wait_ge(ld, 16 * 8)
            for j in range(12):
                for h in range(HALVES):
                    mm = pe.matmul(psum[:, 0, j * B:(j + 1) * B], wmod_sb[:, h, j * P:(j + 1) * P], csil[:, h, :],
                                   start=(h == 0), stop=(h == HALVES - 1))
            for m in range(HALVES):
                for k in range(PAIRS):
                    wo_k = prob[k // 4][:, (k % 4) * D + m * P:(k % 4) * D + (m + 1) * P]
                    mm = pe.matmul(psum[:, 1, m:m + 1], wo_k, bv_t[:, k:k + 1], start=(k == 0), stop=(k == PAIRS - 1))
            mm.then_inc(su_p, 1)
            pe.wait_ge(cst, 2)
            pe.wait_ge(su_d, 8)
            pe.sem_inc(ring_full, OFF_RING)
            pe.sem_inc(pv_done, OFF_S)
            pe.sem_inc(ln_var, 2)
            with pe.Fori(0, B) as b:
                for t in range(KT):
                    pe.wait_ge(x_in[t % 4], b * (16 * (KT // 4)) + 16 * (t // 4 + 1))
                    if t >= 4:
                        pe.wait_ge(tp_free, b * KT + t - 3)
                    for h in range(HALVES):
                        mm = pe.transpose(psum[:, t % 4, h * P:(h + 1) * P], tok[t % 4][:, h * P:(h + 1) * P], identf[:])
                    mm.then_inc(tp_full, 1)
                phase_end(pe, b, PH_LOAD)
                ln_pe(pe, b * LN_B)
                phase_end(pe, b, PH_LN1)

                def ring_slot(rb, r):
                    pe.wait_ge(ring_free, OFF_RING + rb + r + 1)
                    return psum[:, M_BANK + r % 2, :]

                def proj_qk(G, s, i, use):
                    if i == 0:
                        pe.wait_ge(w_in[s], 80 * use)
                    for h in range(HALVES):
                        mm = pe.matmul(psum[:, S_BANK + i, :], wqk_h[s][:, h, :], hT[:, h, i * T:(i + 1) * T],
                                       start=(h == 0), stop=(h == HALVES - 1))
                    mm.then_inc(pj_full, 1)

                def proj_v(G, s, i):
                    pe.wait_ge(pj_dup, G * QK_ITEMS + i + 1)
                    pe.wait_ge(pj_dve, G * PJ_ITEMS + i + 1)
                    for t in range(8):
                        tt = i * 8 + t
                        for h in range(HALVES):
                            mm = pe.matmul(psum[:, S_BANK + i, t * DH:(t + 1) * DH], hT[:, h, tt * P:(tt + 1) * P], wv_h[s][:, h, :],
                                           start=(h == 0), stop=(h == HALVES - 1))
                    mm.then_inc(pj_full, 1)

                def max_tile(rb, r, s, j):
                    qt, c = divmod(j, CHUNKS)
                    ps = ring_slot(rb, r)
                    pe.matmul(ps, qhh[s][0:DH, qt * P:(qt + 1) * P], kh1[s][0:DH, c * T:(c + 1) * T],
                              start=True, stop=True).then_inc(ring_full, 1)

                def turn(G, rb, r):
                    ps = ring_slot(rb, r)
                    pe.wait_ge(mx_red, G + 1)
                    pe.transpose(ps[0:KT, 0:P], mx1[:], identf[:]).then_inc(ring_full, 1)

                def projected(G):
                    pe.wait_ge(pj_dup, G * QK_ITEMS + QK_ITEMS)
                    pe.wait_ge(pj_dve, G * PJ_ITEMS + PJ_ITEMS)

                def scores(G, s, t):
                    cp, kt = divmod(t, KT)
                    keys = slice(kt * P, (kt + 1) * P)
                    for j in range(2):
                        cols = slice((2 * cp + j) * T, (2 * cp + j + 1) * T)
                        ps = psum[:, S_BANK + 2 * (t % 2) + j, :]
                        pe.matmul(ps, klh[s][:, keys], qhh[s][:, cols], start=True, stop=False)
                        mm = pe.matmul(ps, kh1[s][:, keys], qlm[s][:, cols], start=False, stop=True)
                    mm.then_inc(s_full, 1)

                def values(G, s, t):
                    cp, kt = divmod(t, KT)
                    pe.wait_ge(exp_done, G * STEPS + t + 1)
                    if kt == 0:
                        pe.wait_ge(o_free, G * CP + cp + 1)
                    for j in range(2):
                        mm = pe.matmul(psum[j * DH:(j + 1) * DH, O_BANK + cp, :], vv[s][:, kt, :],
                                       prob[t % PRING][:, j * T:(j + 1) * T], start=(kt == 0), stop=(kt == KT - 1))
                    mm.then_inc(pv_done, 1)

                def sums(G, rb, r, cp):
                    ps = ring_slot(rb, r)
                    pe.wait_ge(pool_sum, G * (CP * POOL_OPS) + OFF_POOL + (cp + 1) * POOL_OPS)
                    pe.wait_ge(dve_sum, G * (CP * DVE_OPS) + OFF_DVE + (cp + 1) * DVE_OPS)
                    for a, acc in enumerate((acc_p, acc_d)):
                        for j in range(2):
                            mm = pe.matmul(ps[j * DH:(j + 1) * DH], ones[:], acc[cp][:, j * T:(j + 1) * T],
                                           start=(a == 0), stop=(a == 1))
                    mm.then_inc(ring_full, 1)

                def out_tile(G, rb, r, j, use):
                    c, m = divmod(j, HALVES)
                    ps = ring_slot(rb, r)
                    if j == 0:
                        pe.wait_ge(wo_in, 16 * use)
                        pe.wait_ge(o_free, G * CP + CP + CP)
                    pe.matmul(ps, wo_p[:, m * P:(m + 1) * P], oT[:, c * T:(c + 1) * T], start=True, stop=True).then_inc(ring_full, 1)

                def head(b, hp, hh, plan):
                    G, rb, s = head_index(b, hp, hh), ring_base(b, hp), hh
                    maxima = any(kind == "max" for kind, _, _ in plan)
                    pe.wait_ge(mrow, G * 16 + 32)
                    if maxima:
                        projected(G + 1)
                    for kind, j, r in plan:
                        if kind == "scores":
                            scores(G, s, j)
                        elif kind == "max":
                            max_tile(rb, r, 1 - s, j)
                        elif kind == "values":
                            values(G, s, j)
                        elif kind == "sum":
                            sums(G, rb, r, j)
                        elif kind == "turn":
                            turn(G + 1, rb, r)
                        elif kind == "proj_qk":
                            proj_qk(G + 2, s, j, b * PAIRS + hp + 2)
                        elif kind == "proj_v":
                            proj_v(G + 2, s, j)
                        elif kind == "out":
                            out_tile(G, rb, r, j, b * PAIRS + hp + 1)
                for hh in range(2):
                    if hh:
                        projected(head_index(b, 0, 0))
                    for kind, j in PROLOGUE:
                        if kind == "proj_qk":
                            proj_qk(head_index(b, 0, hh), hh, j, b * PAIRS + 1)
                        else:
                            proj_v(head_index(b, 0, hh), hh, j)
                for j in range(RING_MAX):
                    max_tile(ring_base(b, 0), j, 0, j)
                turn(head_index(b, 0, 0), ring_base(b, 0), RING_MAX)
                projected(head_index(b, 0, 1))
                pe.sem_inc(bar_left, 1)
                with pe.Fori(0, PAIRS - 1) as hp:
                    for hh in range(2):
                        head(b, hp, hh, PLAN[False][hh])
                for hh in range(2):
                    head(b, PAIRS - 1, hh, PLAN[True][hh])
                phase_end(pe, b, PH_ATT)
                ln_pe(pe, b * LN_B + CHUNKS)
                phase_end(pe, b, PH_LN2)
                with pe.Fori(0, LAYERS) as l:
                    n0 = layer_index(b, l) * WINDOWS
                    pe.wait_ge(lw_in, b * LW_B + (l + 1) * LW_L)
                    pe.wait_ge(zp_ok, layer_index(b, l) + 1)
                    pe.wait_ge(msk_ok, b + 1)

                    def project_qk(n, par):
                        pe.wait_ge(hc_ok, n + 1)
                        pe.wait_ge(qkT_read, n + 1)
                        for a in range(2):
                            for h in range(HALVES):
                                mm = pe.matmul(psum[:, QK_B + a, :], hc[par][:, h, :], wqkv_l[:, h, a * INNER:(a + 1) * INNER],
                                               start=(h == 0), stop=(h == HALVES - 1))
                        mm.then_inc(qk_full, 1)

                    def project_v(n, par):
                        pe.wait_ge(vl_read, n + 1)
                        for h in range(HALVES):
                            mm = pe.matmul(psum[:, V_B, :], hc[par][:, h, :], wqkv_l[:, h, 2 * INNER:3 * INNER],
                                           start=(h == 0), stop=(h == HALVES - 1))
                        mm.then_inc(vl_full, 1)

                    def turn_qk(n):
                        pe.wait_ge(rot_done, n + 1)
                        for a in range(2):
                            for p in range(LPAIRS):
                                mm = pe.transpose(psum[:, QK_B + a, p * WIN:(p + 1) * WIN], qk_w[:, a * INNER + p * P:a * INNER + (p + 1) * P], identf[:])
                        mm.then_inc(qkT_full, 1)

                    def local_scores(n, i, par, it):
                        if it == 0:
                            pe.wait_ge(qkT_read, n + 2)
                        pe.wait_ge(lpT_read, n * ITEMS + it + 1)
                        for a in range(2):
                            p = 2 * it + a
                            ps = psum[:, p, :]
                            if par:
                                mask = mask_b[:, WINDOWS // 2:WINDOWS // 2 + 1, :]
                            else:
                                mask = mask_b[:, (slice(i, i + 1) if isinstance(i, int) else bass.ds(i, 1)), :]
                            pe.matmul(ps.rearrange("p (t k) -> p t k", t=2), identb[:], mask.broadcast_to([P, 2, 2 * WIN]),
                                      start=True, stop=False, skip_group_check=True)
                            for o, q in enumerate((q_even, q_odd)):
                                mm = pe.matmul(ps[:, o * 2 * WIN:(o + 1) * 2 * WIN], q[:, p, :], k_l[:, p].rearrange("p s n -> p (s n)"),
                                               start=False, stop=True, skip_group_check=True)
                        mm.then_inc(ls_full, 1)

                    def turn_probs(n, it):
                        pe.wait_ge(lp_done, n * ITEMS + it + 1)
                        for h in range(IH):
                            for half in range(2):
                                j = h * 2 + half
                                mm = pe.transpose(psum[:, 2 * it + j // 4, (j % 4) * P:(j % 4 + 1) * P], lp[:, it * IH + h, half * WIN:(half + 1) * WIN], identf[:])
                        mm.then_inc(lpT_full, 1)

                    def local_values(n, par, it):
                        pe.wait_ge(lpT_read, n * ITEMS + it + 1 + ITEMS)
                        if it == 0:
                            pe.wait_ge(lo_read, n + 1)
                        for p in range(2 * it, 2 * it + 2):
                            for half in range(2):
                                for o in range(2):
                                    h = 2 * p + o
                                    mm = pe.matmul(psum[o * DH:(o + 1) * DH, OL_B, p * WIN:(p + 1) * WIN], v_l[half][:, h * DH:(h + 1) * DH], lpT[:, h, half, :],
                                                   start=(half == 0), stop=(half == 1), skip_group_check=True)
                        if it == 1:
                            mm.then_inc(ol_full, 1)

                    def local_out(n):
                        pe.wait_ge(ol_read, n + 1)
                        for m in range(HALVES):
                            for k in range(LPAIRS):
                                mm = pe.matmul(psum[:, OL_B, m * WIN:(m + 1) * WIN], wo_l[:, k, m * P:(m + 1) * P], oL[:, k, :],
                                               start=(k == 0), stop=(k == LPAIRS - 1))
                        mm.then_inc(lo_full, 1)

                    def pe_prologue():
                        project_qk(n0, 0)
                        project_v(n0, 0)
                        turn_qk(n0)

                    def pe_window(i, par, has_next):
                        n = n0 + i * 2 + par
                        local_scores(n, i, par, 0)
                        local_scores(n, i, par, 1)
                        if has_next:
                            project_qk(n + 1, 1 - par)
                        turn_probs(n, 0)
                        turn_probs(n, 1)
                        local_values(n, par, 0)
                        local_values(n, par, 1)
                        if has_next:
                            project_v(n + 1, 1 - par)
                        local_out(n)
                        if has_next:
                            turn_qk(n + 1)
                    windows(pe, pe_prologue, pe_window)
                    phase_end(pe, b, PH_L0 + l * 2)

                    m0, q0 = layer_index(b, l) * CHUNKS, b * LN_B + 2 * CHUNKS + l * CHUNKS
                    pe.wait_ge(l1_in, (layer_index(b, l) + 1) * (16 * 11))

                    def shifted_src(c):
                        return lambda h: x1[:, h, columns(c * T, T, shifted=h)]

                    def pe_mlp_prologue():
                        ln_mean(pe, q0, shifted_src(0))
                        ln_variance(pe, q0, 0)

                    def pe_chunk(i, par, has_next):
                        c = i * 2 + par
                        m = m0 + c
                        pe.wait_ge(ln_done, q0 + c + 3)

                        def up(t):
                            o, size = HID_TILES[t]
                            pe.wait_ge(ug_done, m * HT + t + 1)
                            for j, bank in ((0, 2 + t % 2), (1, 4 + t % 2)):
                                for h in range(HALVES):
                                    mm = pe.matmul(psum[0:size, bank, :], w1_l[:, h, j * HID + o:j * HID + o + size], hn[par][:, h, :],
                                                   start=(h == 0), stop=(h == HALVES - 1))
                            mm.then_inc(ag_full, 1)

                        def down(t):
                            o, size = HID_TILES[t]
                            pe.wait_ge(ug_done, m * HT + t + 3)
                            if t == 0:
                                pe.wait_ge(y_read, m + 1)
                            for h in range(HALVES):
                                mm = pe.matmul(psum[:, 6 + h, :], w2_l[0:size, t, h * P:(h + 1) * P], ug[t % 3][0:size, :],
                                               start=(t == 0), stop=(t == HT - 1))
                            if t == HT - 1:
                                mm.then_inc(y_full, 1)
                        for t in range(HT):
                            up(t)
                            if t:
                                down(t - 1)
                            if has_next and t == NORM_AT - 1:
                                ln_mean(pe, q0 + c + 1, shifted_src(c + 1))
                            if has_next and t == NORM_AT + 1:
                                ln_variance(pe, q0 + c + 1, 1 - par)
                        down(HT - 1)
                    mlp(pe, pe_mlp_prologue, pe_chunk)
                    phase_end(pe, b, PH_L0 + l * 2 + 1)
                pe.wait_ge(fin_ok, b + 1)
                for t in range(KT):
                    if t >= 4:
                        pe.wait_ge(ot_tok, b * KT + t - 3)
                    for h in range(HALVES):
                        mm = pe.transpose(psum[:, t % 4, h * P:(h + 1) * P], xT[:, h, t * P:(t + 1) * P], identf[:])
                    mm.then_inc(ot_full, 1)
                phase_end(pe, b, PH_STORE)


_INS = ["L0_attn_x", "L0_attn_Wq", "L0_attn_bq", "L0_attn_Wk", "L0_attn_bk", "L0_attn_Wv", "L0_attn_bv", "L0_attn_Wo",
        "L0_attn_bo", "L0_ffn_wqkv", "L0_ffn_q_scale", "L0_ffn_k_scale", "L0_ffn_wo", "L0_ffn_ln_g", "L0_ffn_ln_b",
        "L0_ffn_w1", "L0_ffn_b1", "L0_ffn_w2", "L0_ffn_b2", "L0_c", "L0_wmod"]


def kernel(**inputs):
    import concourse.bacc as bacc
    from concourse.bass_utils import run_bass_kernel_spmd

    nc = bacc.Bacc("TRN2", target_bir_lowering=False, num_devices=1)
    arrays = {n: np.ascontiguousarray(inputs[n]) for n in _INS}
    arrays.update({"const_" + n: a for n, a in shape_constants().items()})
    args = [nc.dram_tensor(n, a.shape, mybir.dt.from_np(a.dtype), kind="ExternalInput").ap() for n, a in arrays.items()]
    out = nc.dram_tensor("out", (B, N, D), F32, kind="ExternalOutput").ap()
    adaln_block(nc, *args, out)
    r = run_bass_kernel_spmd(nc, [arrays], core_ids=[0])
    return r.results[0]["out"]
```

```python
from contextlib import ExitStack

import numpy as np

import concourse.bass as bass
from concourse import mybir

F32 = mybir.dt.float32
F32R = mybir.dt.float32r
BF16 = mybir.dt.bfloat16
ALU = mybir.AluOpType
ACT = mybir.ActivationFunctionType
AX_X = mybir.AxisListType.X

P = 128
B, N, D = 2, 2048, 256
HALVES = D // P
T = 512
CHUNKS = N // T
EPS = 1e-5

HEADS, DH = 16, 64
PAIRS = HEADS // 2
KT = N // P
CP = CHUNKS // 2
STEPS = CP * KT
PRING = 4
SUM_DVE = (2, 5, 8, 12)
SUM_POOL = tuple(k for k in range(KT) if k not in SUM_DVE)
JOIN = -1
POOL_SEQ = SUM_POOL[1:-1] + (JOIN,) + SUM_POOL[-1:]
POOL_OPS = len(POOL_SEQ)
DVE_OPS = len(SUM_DVE)
QK_ITEMS, V_ITEMS = CHUNKS, 4
V_TILES = KT // V_ITEMS
WO_ITEMS = CHUNKS * HALVES
RING_MAX = KT * CHUNKS
RING_PAIR = 2 * (RING_MAX + 1 + CP) + V_ITEMS + WO_ITEMS
RING_PRO = V_ITEMS + RING_MAX + 1
ATT_SCALE = 1.0 / np.sqrt(np.float32(DH))

LAYERS, LHEADS, WIN = 2, 8, 128
INNER = LHEADS * DH
LPAIRS = LHEADS // 2
WINDOWS = N // WIN
ITEMS = 2
IH = LHEADS // ITEMS
HID = int(D * 4 * 2 / 3)
HID_TILES = [(o, min(P, HID - o)) for o in range(0, HID, P)]
HT = len(HID_TILES)
HID_LAST = HID_TILES[-1][1]
HID_COLS = HID + HT * P
QK_SCALE = 8.0
MASKED = -1.0e30


def shape_constants():
    f = np.float32
    eye = np.eye(P, dtype=f)
    half = np.arange(0, DH, 2, dtype=f)
    inv = (f(1.0) / np.power(f(10000.0), half / f(DH))).astype(f)
    t = np.arange(N, dtype=f)
    fr = (t[:, None] * inv[None, :]).astype(f)
    fr = np.concatenate([fr, fr], -1)
    base = ((half + f(0.4 * DH)) / f(1.4 * DH)).astype(f)
    power = ((t - N // 2) / f(WIN // 2)).astype(f)
    sc = np.power(base[None, :].astype(np.float64), power[:, None].astype(np.float64)).astype(f)
    sc = np.concatenate([sc, sc], -1)
    cos, sin = np.cos(fr.astype(np.float64)).astype(f), np.sin(fr.astype(np.float64)).astype(f)
    sign = np.concatenate([-np.ones(DH // 2, f), np.ones(DH // 2, f)])
    tabs = [cos * sc, sin * sc * sign, cos / sc, sin / sc * sign]
    rot = np.stack(tabs, 1).astype(f)
    q, k = np.arange(P)[:, None], np.arange(P)[None, :]
    prev = np.where(k >= q, 0.0, MASKED)
    cur = np.where(k <= q, 0.0, MASKED)
    none = np.full((P, P), MASKED)
    masks = np.stack([np.concatenate([cur, none if w == 0 else prev], 1) for w in range(0, WINDOWS, 2)]
                     + [np.concatenate([prev, cur], 1)], 1).astype(f)
    return {"eye": eye, "rot": rot, "masks": masks}


def adaln_block(nc, x, Wq, bq, Wk, bk, Wv, bv, Wo, bo, wqkv, q_scale, k_scale, wo, ln_g, ln_b, w1, b1, w2, b2,
            c_in, wmod, eye, rot, masks, out):
    ctx = ExitStack()
    with ctx, nc.allow_non_contiguous_dma(reason="small per-feature vectors, a feature a partition"):
        def sb(name, shape, dt=F32, at=ctx):
            return at.enter_context(nc.sbuf_tensor(name, shape, dt))

        def sem(name):
            return ctx.enter_context(nc.semaphore(name))

        xT = sb("xT", [P, HALVES, N])
        identf = sb("identf", [P, P])
        ones_ln = sb("ones_ln", [P, P])
        ones = sb("ones", [P, DH])
        mod = sb("mod", [P, 12, B])
        modb = sb("modb", [P, 12])
        csil = sb("csil", [P, HALVES, B])
        gsign = sb("gsign", [P, 2, HALVES, B])
        gsize = sb("gsize", [P, 2, HALVES, B])
        bo_t = sb("bo_t", [P, HALVES])
        bo_all = sb("bo_all", [P, HALVES])
        gabo = sb("gabo", [P, HALVES])
        epst = sb("epst", [P, 1])
        exp_of_eps = sb("exp_of_eps", [P, 1])
        minus_half = sb("minus_half", [P, 1])
        bv_t = sb("bv_t", [P, PAIRS])

        norms = ExitStack()
        lnc = [sb(f"lnc{i}", [P, HALVES, T], at=norms) for i in range(2)]
        lns = [sb(f"lns{i}", [P, HALVES, T], at=norms) for i in range(2)]
        norms.close()
        wqkv_h = [sb(f"w{n}_h", [P, HALVES, T], F32R) for n in "qkv"]
        sb("norms_rest", [P, HALVES, T])
        lnr = [sb(f"lnr{i}", [P, T]) for i in range(2)]
        tok = [sb(f"tok{i}", [P, D]) for i in range(4)]

        att = ExitStack()
        hT = sb("hT", [P, HALVES, N], at=att)
        qhh = [sb(f"qhh{s}", [P, N], F32R, at=att) for s in range(2)]
        qlm = [sb(f"qlm{s}", [DH + 1, N], F32R, at=att) for s in range(2)]
        klh = [sb(f"klh{s}", [P, N], F32R, at=att) for s in range(2)]
        kh1 = [sb(f"kh1{s}", [DH + 1, N], F32R, at=att) for s in range(2)]
        vv = sb("vv", [P, KT, P], at=att)
        wqk_h = [sb(f"wqk{s}", [P, HALVES, P], at=att) for s in range(2)]
        wv_p = sb("wv_p", [P, HALVES, P], at=att)
        bqk_h = [sb(f"bqk{s}", [P, 1], at=att) for s in range(2)]
        wo_p = sb("wo_p", [P, D], at=att)
        prob = [sb(f"prob{i}", [P, 2 * T], at=att) for i in range(PRING)]
        acc_p = [sb(f"accp{i}", [P, 2 * T], at=att) for i in range(CP)]
        acc_d = [sb(f"accd{i}", [P, 2 * T], at=att) for i in range(CP)]
        rcp = sb("rcp", [P, T], at=att)
        oT = sb("oT", [P, N], at=att)
        mx4 = sb("mx4", [P, KT, CHUNKS], at=att)
        mx1 = sb("mx1", [P, KT], at=att)
        nmx = sb("nmx", [KT, P], F32R, at=att)
        wmod_sb = hT[:, :, 0:6 * D]
        att.close()

        ffn = ExitStack()
        xf = sb("xf", [P, HALVES, N + 1], at=ffn)
        x1 = sb("x1", [P, HALVES, N + 1], at=ffn)
        raw = ExitStack()
        wqkv_l = sb("wqkv_l", [P, HALVES, 3 * INNER], at=raw)
        raw.close()
        wqkv_low = sb("wqkv_low", [P, HALVES, 3 * INNER], F32R, at=ffn)
        wo_l = sb("wo_l", [P, LPAIRS, D], at=ffn)
        raw = ExitStack()
        w1_l = sb("w1_l", [P, HALVES, HID_COLS], at=raw)
        w2_l = sb("w2_l", [P, HT, D], at=raw)
        raw.close()
        w1_low = sb("w1_low", [P, HALVES, HID_COLS], F32R, at=ffn)
        w2_low = sb("w2_low", [P, HT, D], F32R, at=ffn)
        w1_h = sb("w1_h", [P, HALVES, HID_COLS], F32R, at=ffn)
        w2_h = sb("w2_h", [P, HT, D], F32R, at=ffn)
        vec_g = sb("vec_g", [P, HALVES], at=ffn)
        vec_b = sb("vec_b", [P, HALVES], at=ffn)
        vec_b1 = sb("vec_b1", [P, 2, HT], at=ffn)
        vec_b2 = sb("vec_b2", [P, HALVES], at=ffn)
        rot_l = sb("rot_l", [P, WINDOWS, 4, DH], at=ffn)
        scales = sb("scales", [P, 4, DH], at=ffn)
        mask_b = sb("mask_b", [P, WINDOWS // 2 + 1, 2 * WIN], BF16, at=ffn)
        identb = sb("identb", [P, P], BF16, at=ffn)
        q_even = sb("q_even", [P, LPAIRS, WIN], at=ffn)
        q_odd = sb("q_odd", [P, LPAIRS, WIN], at=ffn)
        both = ExitStack()
        hc_h = [sb(f"hc_h{i}", [P, HALVES, WIN], F32R, at=both) for i in range(2)]
        hc_l = [sb(f"hc_l{i}", [P, HALVES, WIN], F32R, at=both) for i in range(2)]
        qk_sq = sb("qk_sq", [P, 2 * INNER], at=both)
        qk_u = sb("qk_u", [P, 2 * INNER], at=both)
        qk_w = sb("qk_w", [P, 2 * INNER], at=both)
        ssq = sb("ssq", [P, 2 * LHEADS], at=both)
        ssc = sb("ssc", [P, 2 * LHEADS], at=both)
        rnorm = sb("rnorm", [P, 2 * LHEADS], at=both)
        k_l = sb("k_l", [P, LPAIRS, 2, WIN], at=both)
        v_l = [sb(f"v_l{i}", [P, INNER], at=both) for i in range(2)]
        lp = sb("lp", [P, LHEADS, 2 * WIN], at=both)
        lpT = sb("lpT", [P, LHEADS, 2, WIN], at=both)
        lmax = sb("lmax", [P, LHEADS], at=both)
        lneg = sb("lneg", [P, LHEADS], at=both)
        lsum = sb("lsum", [P, LHEADS], at=both)
        lrcp = sb("lrcp", [P, LHEADS], at=both)
        oL = sb("oL", [P, LPAIRS, WIN], at=both)
        both.close()
        hn_h = [sb(f"hn_h{i}", [P, HALVES, T], F32R, at=ffn) for i in range(2)]
        hn_l = [sb(f"hn_l{i}", [P, HALVES, T], F32R, at=ffn) for i in range(2)]
        gl = [sb(f"gl{i}", [P, T], at=ffn) for i in range(2)]
        uf = [sb(f"uf{i}", [P, T], at=ffn) for i in range(2)]
        ug_h = [sb(f"ug_h{i}", [P, T], F32R, at=ffn) for i in range(3)]
        ug_l = [sb(f"ug_l{i}", [P, T], F32R, at=ffn) for i in range(3)]
        ffn.close()

        psum = ctx.enter_context(nc.psum_tensor("psum", [P, 8, T], F32))
        QK_B, V_B, OL_B, NORM_AT = 4, 6, 7, 3
        S_BANK, O_BANK, M_BANK = 0, 4, 6

        ld = sem("ld")
        cst = sem("cst")
        su_a, su_p, su_d = sem("su_a"), sem("su_p"), sem("su_d")
        bar = sem("bar")
        bar_left = sem("bar_left")
        x_in = [sem(f"x_in{i}") for i in range(4)]
        tp_full, tp_free = sem("tp_full"), sem("tp_free")
        ln_mu, ln_c, ln_sq, ln_var, ln_sd, ln_done = (sem("ln_" + s) for s in ("mu", "c", "sq", "var", "sd", "done"))
        ln_r = sem("ln_r")
        w_in = [sem(f"w_in{s}") for s in range(2)]
        wo_in, wv_in = sem("wo_in"), sem("wv_in")
        pj_full, pj_hi, pj_dup, pj_dve = sem("pj_full"), sem("pj_hi"), sem("pj_dup"), sem("pj_dve")
        ring_full, ring_free = sem("ring_full"), sem("ring_free")
        s_full, exp_done, pv_done = sem("s_full"), sem("exp_done"), sem("pv_done")
        pool_sum, dve_sum = sem("pool_sum"), sem("dve_sum")
        o_free, oT_ready = sem("o_free"), sem("oT_ready")
        mx_red, mrow = sem("mx_red"), sem("mrow")
        rcp_ok = sem("rcp_ok")
        mod_ok, x_ok = sem("mod_ok"), sem("x_ok")
        ot_full, ot_tok = sem("ot_full"), sem("ot_tok")
        stored = [sem(f"stored{i}") for i in range(4)]

        mask_f_view = x1[:].rearrange("p h n -> p (h n)")[:, 0:(WINDOWS // 2 + 1) * 2 * WIN].rearrange("p (m k) -> p m k", k=2 * WIN)
        lw_in, l1_in, msk_in, msk_ok = sem("lw_in"), sem("l1_in"), sem("msk_in"), sem("msk_ok")
        rot_ok, zp_ok = sem("rot_ok"), sem("zp_ok")
        hc_ok, qk_full, vl_full, sq_done, ss_done, rn_done = (sem(n) for n in ("hc_ok", "qk_full", "vl_full", "sq_done", "ss_done", "rn_done"))
        ru_done, rot_done, qkT_full, qkT_read, vl_read, pc_done = (sem(n) for n in ("ru_done", "rot_done", "qkT_full", "qkT_read", "vl_read", "pc_done"))
        ls_full, lmx_done, lneg_done, lexp_done, lrcp_done, lp_done = (sem(n) for n in ("ls_full", "lmx_done", "lneg_done", "lexp_done", "lrcp_done", "lp_done"))
        lpT_full, lpT_read, ol_full, ol_read, lo_full, lo_read = (sem(n) for n in ("lpT_full", "lpT_read", "ol_full", "ol_read", "lo_full", "lo_read"))
        ag_full, gelu_done, ug_done, y_read = (sem(n) for n in ("ag_full", "gelu_done", "ug_done", "y_read"))
        hc_hi, wa_hi, wa_lo = sem("hc_hi"), sem("wa_hi"), sem("wa_lo")
        w_hi, w_lo, hn_hi, ug_hi, ug_lo, down_done = (sem(n) for n in ("w_hi", "w_lo", "hn_hi", "ug_hi", "ug_lo", "down_done"))
        fin_ok = sem("fin_ok")

        block = ctx.enter_context(nc.Block())

        PH_LOAD, PH_LN1, PH_ATT, PH_LN2, PH_L0, PH_STORE, PH = 0, 1, 2, 3, 4, 8, 9

        GROUPS = STEPS // 2
        SUM0_GROUP = (KT + 5) // 2

        def max_places(outs):
            weight = [4] * (GROUPS - 1) + [0]
            weight[0] = 1
            weight[SUM0_GROUP + 1:SUM0_GROUP + 3] = [0, 2]
            for g in outs:
                weight[g] = 3
            return [-(-RING_MAX * sum(weight[:g + 1]) // sum(weight)) for g in range(GROUPS)]

        def head_order(first, last, hh):
            maxima, projects = not (last and hh), not last
            outs = () if first or hh else range(1, 1 + WO_ITEMS // 2)
            placed = max_places(outs)
            order = [("scores", 0), ("scores", 1)]
            for g in range(GROUPS):
                upto = placed[g] if maxima else 0
                done = (placed[g - 1] if g else 0) if maxima else 0
                tiles = [("max", j) for j in range(done, upto)]
                if g in outs:
                    tiles += [("out", 2 * (g - 1)), ("out", 2 * (g - 1) + 1)]
                n = len(tiles)
                cut0 = (n + 1) // 3
                cut1 = cut0 + n // 3
                if g + 1 < GROUPS:
                    order += tiles[:cut0] + [("scores", 2 * g + 2)] + tiles[cut0:cut1] + [("scores", 2 * g + 3)] + tiles[cut1:]
                else:
                    if maxima:
                        order.append(("turn", 0))
                    if projects:
                        order += [("proj_qk", i) for i in range(QK_ITEMS)]
                order += [("values", 2 * g), ("values", 2 * g + 1)]
                if g == SUM0_GROUP:
                    order.append(("sum", 0))
            if projects and hh == 1:
                order += [("proj_v", i) for i in range(V_ITEMS)]
            order.append(("sum", 1))
            if last and hh:
                order += [("out", j) for j in range(WO_ITEMS)]
            return order

        IN_RING = ("max", "turn", "sum", "out", "proj_v")

        def pair_plan(first, last):
            plans, r = [], RING_PRO if first else RING_PRO - WO_ITEMS
            for hh in range(2):
                rows = []
                for kind, j in head_order(first, last, hh):
                    rows.append((kind, j, r))
                    r += kind in IN_RING
                plans.append(rows)
            assert r == RING_PAIR + (0 if last else RING_PRO - WO_ITEMS)
            return plans

        FIRST, MIDDLE, LAST = 0, 1, 2
        PLAN = [pair_plan(True, False), pair_plan(False, False), pair_plan(False, True)]
        VALUES_READ = RING_PRO - WO_ITEMS - 1

        def place(which, hh, kind):
            return [r for k, _, r in PLAN[which][hh] if k == kind][-1]

        def head_index(b, hp, hh):
            return b * HEADS + hp * 2 + hh

        def ring_base(b, hp):
            return b * (RING_PAIR * PAIRS) + hp * RING_PAIR

        OFF_S, OFF_POOL, OFF_DVE, OFF_RING = STEPS, CP * POOL_OPS, CP * DVE_OPS, RING_PAIR

        def pool_used(kt):
            return 1 if kt == SUM_POOL[0] else POOL_SEQ.index(kt) + 1

        def phase_end(eng, b, phase):
            eng.drain().then_inc(bar, 1)
            eng.wait_ge(bar, b * (5 * PH) + 5 * (phase + 1))
            eng.sem_inc(bar_left, 1)

        LW_L = 16 * 10
        LW_B = LW_L * (1 + LAYERS)
        LN_B = CHUNKS * (2 + LAYERS)

        def ln_mean(pe, n, src):
            pe.wait_ge(ln_c, n + 1)
            for h in range(HALVES):
                mm = pe.matmul(psum[:, 0, :], ones_ln[:], src(h), start=(h == 0), stop=(h == HALVES - 1))
            mm.then_inc(ln_mu, 1)

        def ln_variance(pe, n, par):
            pe.wait_ge(ln_sq, n + 1)
            pe.wait_ge(ln_sd, n + 1)
            for h in range(HALVES):
                mm = pe.matmul(psum[:, 1, :], ones_ln[:], lns[par][:, h, :], start=(h == 0), stop=(h == HALVES - 1))
            mm.then_inc(ln_var, 1)

        def ln_square(act, n, par):
            act.wait_ge(ln_c, n + 2)
            act.wait_ge(ln_var, n + 1)
            act.activation(lns[par][:], lnc[par][:], ACT.Square).then_inc(ln_sq, 1)

        def ln_deviation(act, n, par):
            act.wait_ge(ln_var, n + 3)
            act.wait_ge(ln_done, n + 1)
            act.activation(lnr[par][:], psum[:, 1, :], ACT.Sqrt, bias=epst[:, 0:1]).then_inc(ln_sd, 1)

        def ln_centre(dve, n, par, src):
            dve.wait_ge(ln_mu, n + 1)
            dve.wait_ge(ln_done, n + 1)
            for h in range(HALVES):
                op = dve.tensor_tensor(lnc[par][:, h, :], src(h), psum[:, 0, :], ALU.subtract)
            op.then_inc(ln_c, 1)

        def ln_inverse(dve, n, par):
            dve.wait_ge(ln_sd, n + 2)
            dve.wait_ge(ln_sq, n + 1)
            dve.reciprocal(lnr[par][:], lnr[par][:]).then_inc(ln_r, 1)

        def ln_gain(dve, n, par, gain):
            dve.wait_ge(ln_r, n * 3 + 1)
            for h in range(HALVES):
                dve.scalar_tensor_tensor(lnc[par][:, h, :], lnc[par][:, h, :], gain(h), lnr[par][:],
                                         ALU.mult, ALU.mult).then_inc(ln_r, 1)
            dve.wait_ge(ln_r, n * 3 + 3)

        def ln_scale(dve, n, par, dst, gain, shift):
            ln_inverse(dve, n, par)
            ln_gain(dve, n, par, gain)
            for h in range(HALVES):
                op = dve.tensor_scalar(dst(h), lnc[par][:, h, :], shift(h), None, ALU.add)
            op.then_inc(ln_done, 1)

        def xt(c):
            return lambda h: xT[:, h, c * T:(c + 1) * T]

        def ln_pe(pe, n0):
            ln_mean(pe, n0, xt(0))
            for c in range(CHUNKS):
                if c + 1 < CHUNKS:
                    ln_mean(pe, n0 + c + 1, xt(c + 1))
                ln_variance(pe, n0 + c, c % 2)

        def ln_act(act, n0):
            ln_square(act, n0, 0)
            for c in range(CHUNKS):
                if c + 1 < CHUNKS:
                    ln_square(act, n0 + c + 1, (c + 1) % 2)
                ln_deviation(act, n0 + c, c % 2)

        def ln_dve(dve, n0, dst, gain, shift):
            ln_centre(dve, n0, 0, xt(0))
            for c in range(CHUNKS):
                if c + 1 < CHUNKS:
                    ln_centre(dve, n0 + c + 1, (c + 1) % 2, xt(c + 1))
                ln_scale(dve, n0 + c, c % 2, dst(c), gain, shift)

        def layer_index(b, l):
            return b * LAYERS + l

        def columns(t0, size, shifted=0):
            start = t0 + (1 - shifted)
            return slice(start, start + size) if isinstance(start, int) else bass.ds(start, size)

        def windows(eng, prologue, body):
            prologue()
            for par in range(2):
                body(0, par, par == 1, True, True)
            with eng.Fori(1, WINDOWS // 2 - 1) as i:
                for par in range(2):
                    body(i, par, True, True, True)
            for par in range(2):
                body(WINDOWS // 2 - 1, par, True, par == 0, False)

        def mlp(eng, prologue, chunk):
            prologue()
            with eng.Fori(0, CHUNKS // 2 - 1) as i:
                for par in range(2):
                    chunk(i, par, True)
            for par in range(2):
                chunk(CHUNKS // 2 - 1, par, par == 0)

        @block.sync
        def _(sp):
            for dst, src in ((identf[:], eye), (bo_t[:], bo.rearrange("(m p) -> p m", p=P)),
                             (bv_t[:], bv.rearrange("(m p) -> p m", p=P)),
                             (csil[:, 0, :], c_in[:, 0:P].rearrange("b p -> p b")),
                             (csil[:, 1, :], c_in[:, P:D].rearrange("b p -> p b")),
                             (wmod_sb, wmod.rearrange("(h p) n -> p h n", p=P)),
                             ):
                sp.dma_start(dst, src).then_inc(ld, 16)
            sp.dma_start(prob[0][:].rearrange("p (m n) -> p m n", n=D), Wo[0:4 * P, :].rearrange("(m p) n -> p m n", p=P)).then_inc(ld, 16)
            sp.dma_start(prob[1][:].rearrange("p (m n) -> p m n", n=D), Wo[4 * P:8 * P, :].rearrange("(m p) n -> p m n", p=P)).then_inc(ld, 16)
            sp.sem_inc(mrow, 16)
            with sp.Fori(0, B) as b:
                for t in range(KT):
                    if t >= 4:
                        sp.wait_ge(tp_full, b * KT + (t - 4) + 1)
                    sp.dma_start(tok[t % 4][:], x[bass.ds(b, 1), t * P:(t + 1) * P, :].rearrange("o p d -> (o p) d")).then_inc(x_in[t % 4], 16)
                phase_end(sp, b, PH_LOAD)
                phase_end(sp, b, PH_LN1)

                def load_head(hexpr, s):
                    cols = slice(hexpr * DH, hexpr * DH + DH) if isinstance(hexpr, int) else bass.ds(hexpr * DH, DH)
                    for w, lo in ((Wq, 0), (Wk, DH)):
                        sp.dma_start(wqk_h[s][:, :, lo:lo + DH], w[:, cols].rearrange("(h p) n -> p h n", p=P)).then_inc(w_in[s], 16)
                    sp.dma_start(bqk_h[s][0:DH, :], bq[cols].rearrange("(p o) -> p o", o=1)).then_inc(w_in[s], 16)
                    sp.dma_start(bqk_h[s][DH:P, :], bk[cols].rearrange("(p o) -> p o", o=1)).then_inc(w_in[s], 16)

                def load_wo(hp):
                    sp.dma_start(wo_p[:], Wo[bass.ds(hp * P, P), :]).then_inc(wo_in, 16)

                def load_wv(hp):
                    cols = slice(hp * P, hp * P + P) if isinstance(hp, int) else bass.ds(hp * P, P)
                    sp.dma_start(wv_p[:], Wv[:, cols].rearrange("(h p) n -> p h n", p=P)).then_inc(wv_in, 16)

                def store_max(b, hp, at, s):
                    sp.wait_ge(ring_free, OFF_RING + 2 + ring_base(b, hp) + at + 1)
                    sp.dma_start(qlm[s][DH:DH + 1, :].bitcast(F32).rearrange("o (t p) -> o t p", p=P),
                                 nmx[:].bitcast(F32)).then_inc(mrow, 16)

                def free_head(b, hp, hh):
                    sp.wait_ge(pj_dup, head_index(b, hp, hh) * QK_ITEMS + QK_ITEMS)
                    sp.wait_ge(pj_dve, head_index(b, hp, hh) * QK_ITEMS + QK_ITEMS)

                def pair(b, hp, which):
                    if which != LAST:
                        sp.wait_ge(ring_full, OFF_RING + ring_base(b, hp) + VALUES_READ)
                        load_wv(hp + 1)
                        for hh in range(2):
                            free_head(b, hp, hh)
                            load_head(hp * 2 + 2 + hh, hh)
                    if which != FIRST:
                        sp.wait_ge(ring_full, OFF_RING + ring_base(b, hp) + place(which, 0, "out") + 1)
                    load_wo(hp)
                    store_max(b, hp, place(which, 0, "turn"), 1)
                    if which != LAST:
                        store_max(b, hp, place(which, 1, "turn"), 0)
                load_head(0, 0)
                load_wv(0)
                load_head(1, 1)
                store_max(b, 0, RING_PRO - 1, 0)
                pair(b, 0, FIRST)
                with sp.Fori(1, PAIRS - 1) as hp:
                    pair(b, hp, MIDDLE)
                pair(b, PAIRS - 1, LAST)
                sp.wait_ge(mrow, b * (16 * HEADS) + 16 + 16 * HEADS)
                sp.sem_inc(bar_left, 1)
                phase_end(sp, b, PH_ATT)
                sp.dma_start(mask_f_view, masks).then_inc(msk_in, 16)

                def load_attention(l):
                    at_l = slice(l, l + 1) if isinstance(l, int) else bass.ds(l, 1)
                    sp.dma_start(rot_l[:], rot.rearrange("(w p) t d -> p w t d", p=P)).then_inc(lw_in, 16)
                    for h in range(HALVES):
                        sp.dma_start(wqkv_l[:, h, :], wqkv[at_l, h * P:(h + 1) * P, :].rearrange("o p n -> (o p) n")).then_inc(lw_in, 16)
                    sp.dma_start(wo_l[:], wo[at_l].rearrange("o (k p) n -> p (o k) n", p=P)).then_inc(lw_in, 16)
                    for j, v in ((0, q_scale), (2, k_scale)):
                        row = v[at_l, :]
                        sp.dma_start(scales[:, j, :], row.broadcast_to([P, DH])).then_inc(lw_in, 16)
                        for o in range(2):
                            sp.dma_start(scales[:, j + 1, o * 32:(o + 1) * 32], row[:, (1 - o) * 32:(2 - o) * 32].broadcast_to([P, 32])).then_inc(lw_in, 16)

                def load_mlp(l):
                    at_l = bass.ds(l, 1)
                    for h in range(HALVES):
                        sp.dma_start(w1_l[:, h, 0:2 * HID], w1[at_l, h * P:(h + 1) * P, :].rearrange("o p n -> (o p) n")).then_inc(l1_in, 16)
                    full = (HT - 1) * P
                    sp.dma_start(w2_l[:, 0:HT - 1, :], w2[at_l, 0:full, :].rearrange("o (k p) n -> p (o k) n", p=P)).then_inc(l1_in, 16)
                    sp.dma_start(w2_l[0:HID - full, HT - 1, :], w2[at_l, full:HID, :].rearrange("o p n -> (o p) n")).then_inc(l1_in, 16)
                    for dst, src in ((vec_g, ln_g), (vec_b, ln_b), (vec_b2, b2)):
                        sp.dma_start(dst[:], src[at_l, :].rearrange("o (h p) -> p (o h)", p=P)).then_inc(l1_in, 16)
                    for j in range(2):
                        sp.dma_start(vec_b1[:, j, 0:HT - 1], b1[at_l, j * HID:j * HID + full].rearrange("o (k p) -> p (o k)", p=P)).then_inc(l1_in, 16)
                        sp.dma_start(vec_b1[0:HID - full, j, HT - 1:HT], b1[at_l, j * HID + full:(j + 1) * HID].rearrange("o p -> p o")).then_inc(l1_in, 16)
                load_attention(0)
                phase_end(sp, b, PH_LN2)
                with sp.Fori(0, LAYERS) as l:
                    load_mlp(l)
                    phase_end(sp, b, PH_L0 + l * 2)
                    load_attention(LAYERS - 1)
                    phase_end(sp, b, PH_L0 + l * 2 + 1)
                for t in range(KT):
                    sp.wait_ge(ot_tok, b * KT + t + 1)
                    sp.dma_start(out[bass.ds(b, 1), t * P:(t + 1) * P, :].rearrange("o p d -> (o p) d"), tok[t % 4][:]).then_inc(stored[t % 4], 16)
                for i in range(4):
                    sp.wait_ge(stored[i], b * (4 * KT) + 4 * KT)
                sp.sem_inc(bar_left, 1)
                phase_end(sp, b, PH_STORE)

        @block.gpsimd
        def _(pool):
            pool.memset(ones_ln[:], 1.0 / D)
            pool.memset(ones[:], 1.0)
            pool.memset(epst[:], EPS).then_inc(cst, 1)
            pool.wait_ge(cst, 1)
            pool.memset(minus_half[:], -0.5).then_inc(cst, 1)
            pool.wait_ge(cst, 2)
            pool.sem_inc(pool_sum, OFF_POOL)
            pool.sem_inc(ug_lo, 2)
            with pool.Fori(0, B) as b:
                phase_end(pool, b, PH_LOAD)
                phase_end(pool, b, PH_LN1)

                def head_sums(G):
                    for cp in range(CP):
                        for i, kt in enumerate(POOL_SEQ):
                            n = G * (CP * POOL_OPS) + OFF_POOL + cp * POOL_OPS + i
                            pool.wait_ge(pool_sum, n)
                            if kt == JOIN:
                                pool.wait_ge(dve_sum, G * (CP * DVE_OPS) + OFF_DVE + (cp + 1) * DVE_OPS)
                                pool.tensor_tensor(acc_p[cp][:], acc_p[cp][:], acc_d[cp][:], ALU.add).then_inc(pool_sum, 1)
                                continue
                            pool.wait_ge(exp_done, G * STEPS + cp * KT + kt + 1)
                            first = acc_p[cp] if i else prob[SUM_POOL[0] % PRING]
                            pool.tensor_tensor(acc_p[cp][:], first[:], prob[kt % PRING][:], ALU.add).then_inc(pool_sum, 1)

                with pool.Fori(0, PAIRS) as hp:
                    for hh in range(2):
                        head_sums(head_index(b, hp, hh))
                phase_end(pool, b, PH_ATT)
                phase_end(pool, b, PH_LN2)
                with pool.Fori(0, LAYERS) as l:
                    n0 = layer_index(b, l) * WINDOWS

                    def inverse_norm(n):
                        pool.wait_ge(ss_done, n * 2 + 2)
                        pool.tensor_tensor(rnorm[:], ssc[:], minus_half[:, 0:1].broadcast_to([P, 2 * LHEADS]), ALU.pow).then_inc(rn_done, 1)

                    def rotate_add(n):
                        pool.wait_ge(ru_done, n * 2 + 1)
                        pool.tensor_tensor(qk_u[:], qk_u[:], qk_w[:], ALU.add).then_inc(ru_done, 1)

                    def scale_probs(n, it):
                        pool.wait_ge(lrcp_done, n * ITEMS + it + 1)
                        hs = slice(it * IH, (it + 1) * IH)
                        pool.tensor_tensor(lp[:, hs, :], lp[:, hs, :], lrcp[:, hs].unsqueeze(2).broadcast_to([P, IH, 2 * WIN]), ALU.mult).then_inc(lp_done, 1)

                    def pool_prologue():
                        inverse_norm(n0)
                        rotate_add(n0)
                        inverse_norm(n0 + 1)
                        rotate_add(n0 + 1)

                    def pool_window(i, par, before, next1, next2):
                        n = n0 + i * 2 + par
                        scale_probs(n, 0)
                        scale_probs(n, 1)
                        if next2:
                            inverse_norm(n + 2)
                            rotate_add(n + 2)
                    windows(pool, pool_prologue, pool_window)
                    pool.wait_ge(w_hi, layer_index(b, l) * 2 + 1)
                    pool.tensor_tensor(w1_low[:, :, 0:2 * HID], w1_l[:, :, 0:2 * HID], w1_h[:, :, 0:2 * HID], ALU.subtract).then_inc(w_lo, 1)
                    pool.wait_ge(w_hi, layer_index(b, l) * 2 + 2)
                    pool.tensor_tensor(w2_low[:, 0:HT - 1, :], w2_l[:, 0:HT - 1, :], w2_h[:, 0:HT - 1, :], ALU.subtract).then_inc(w_lo, 1)
                    pool.wait_ge(w_lo, layer_index(b, l) * 3 + 2)
                    pool.tensor_tensor(w2_low[0:HID_LAST, HT - 1, :], w2_l[0:HID_LAST, HT - 1, :], w2_h[0:HID_LAST, HT - 1, :], ALU.subtract).then_inc(w_lo, 1)
                    phase_end(pool, b, PH_L0 + l * 2)

                    def gated_low(k, t, size):
                        pool.wait_ge(ug_hi, k + 1)
                        pool.wait_ge(ug_lo, k + 2)
                        pool.tensor_tensor(ug_l[t % 3][0:size, :], uf[t % 2][0:size, :], ug_h[t % 3][0:size, :], ALU.subtract).then_inc(ug_lo, 1)

                    with pool.Fori(0, CHUNKS) as c:
                        for t, (o, size) in enumerate(HID_TILES):
                            gated_low((layer_index(b, l) * CHUNKS + c) * HT + t, t, size)
                    phase_end(pool, b, PH_L0 + l * 2 + 1)
                phase_end(pool, b, PH_STORE)

        @block.scalar
        def _(act):
            act.wait_ge(ld, 16 * 8)
            act.activation(csil[:], csil[:], ACT.Silu).then_inc(su_a, 1)
            for s, n in ((ln_sd, 1), (qkT_read, 1), (vl_read, 1), (lpT_read, ITEMS)):
                act.sem_inc(s, n)
            with act.Fori(0, B) as b:
                for t in range(KT):
                    act.wait_ge(tp_full, b * KT + t + 1)
                    act.activation(xT[:, :, t * P:(t + 1) * P], psum[:, t % 4, 0:D].rearrange("p (h n) -> p h n", h=HALVES),
                                   ACT.Copy).then_inc(tp_free, 1)
                phase_end(act, b, PH_LOAD)
                ln_act(act, b * LN_B)
                phase_end(act, b, PH_LN1)

                def project(G, s):
                    for i in range(QK_ITEMS):
                        cols = slice(i * T, (i + 1) * T)
                        ps = psum[:, S_BANK + i % 4, :]
                        act.wait_ge(pj_full, G * QK_ITEMS + i + 1)
                        act.activation(qhh[s][0:DH, cols], ps[0:DH], ACT.Identity, bias=bqk_h[s][0:DH, 0:1])
                        act.activation(klh[s][DH:P, cols], ps[DH:P], ACT.Identity, bias=bqk_h[s][DH:P, 0:1]).then_inc(pj_hi, 1)
                        act.wait_ge(pj_hi, G * QK_ITEMS + i + 1)
                        act.activation(qhh[s][DH:P, cols], qhh[s][0:DH, cols], ACT.Copy).then_inc(pj_dup, 1)

                def exps(G):
                    for t in range(STEPS):
                        act.wait_ge(s_full, G * STEPS + t + 1)
                        act.wait_ge(pv_done, G * STEPS + OFF_S + t - PRING + 1)
                        cp, kt = divmod(t - PRING, KT)
                        if kt in SUM_DVE:
                            act.wait_ge(dve_sum, G * (CP * DVE_OPS) + OFF_DVE + cp * DVE_OPS + SUM_DVE.index(kt) + 1)
                        else:
                            act.wait_ge(pool_sum, G * (CP * POOL_OPS) + OFF_POOL + cp * POOL_OPS + pool_used(kt))
                        act.activation(prob[t % PRING][:], psum[:, S_BANK + 2 * (t % 2):S_BANK + 2 * (t % 2) + 2, :].rearrange("p a b -> p (a b)"),
                                       ACT.Exp, scale=float(ATT_SCALE)).then_inc(exp_done, 1)
                project(head_index(b, 0, 0), 0)
                project(head_index(b, 0, 1), 1)
                with act.Fori(0, PAIRS - 1) as hp:
                    act.activation(exp_of_eps[:], epst[:], ACT.Exp)
                    for hh in range(2):
                        exps(head_index(b, hp, hh))
                        project(head_index(b, hp + 1, hh), hh)
                for hh in range(2):
                    exps(head_index(b, PAIRS - 1, hh))
                phase_end(act, b, PH_ATT)
                ln_act(act, b * LN_B + CHUNKS)
                phase_end(act, b, PH_LN2)
                with act.Fori(0, LAYERS) as l:
                    n0 = layer_index(b, l) * WINDOWS

                    def square(n):
                        act.wait_ge(qk_full, n + 1)
                        act.activation(qk_sq[:], psum[:, QK_B:QK_B + 2, :].rearrange("p a n -> p (a n)"), ACT.Square).then_inc(sq_done, 1)

                    def read_turned(n, par):
                        act.wait_ge(qkT_full, n + 1)
                        qT = psum[:, QK_B, :].rearrange("p (m n) -> p m n", n=WIN)
                        act.activation(q_even[0:DH], qT[0:DH], ACT.Copy)
                        act.activation(q_odd[DH:P], qT[DH:P], ACT.Copy)
                        act.activation(k_l[:, :, par, :], psum[:, QK_B + 1, :].rearrange("p (m n) -> p m n", n=WIN), ACT.Copy).then_inc(qkT_read, 1)

                    def read_values(n, par):
                        act.wait_ge(vl_full, n + 1)
                        act.activation(v_l[par][:], psum[:, V_B, :], ACT.Copy).then_inc(vl_read, 1)

                    def exp_item(n, it):
                        act.wait_ge(lneg_done, n * ITEMS + it + 1)
                        for h in range(IH):
                            hh = it * IH + h
                            op = act.activation(lp[:, hh, :], psum[:, 2 * it + h // 2, (h % 2) * 2 * WIN:(h % 2 + 1) * 2 * WIN], ACT.Exp,
                                                bias=lneg[:, hh:hh + 1], scale=QK_SCALE, accum_out=lsum[:, hh:hh + 1])
                        op.then_inc(lexp_done, 1)

                    def read_probs(n, it):
                        act.wait_ge(lpT_full, n * ITEMS + it + 1)
                        act.activation(lpT[:, it * IH:(it + 1) * IH].rearrange("p h s n -> p (h s n)"),
                                       psum[:, 2 * it:2 * it + 2, :].rearrange("p a n -> p (a n)"), ACT.Copy).then_inc(lpT_read, 1)

                    def split_weights(part):
                        if part == 0:
                            act.wait_ge(l1_in, (layer_index(b, l) + 1) * (16 * 11))
                            act.activation(w1_h[:, :, 0:2 * HID], w1_l[:, :, 0:2 * HID], ACT.Copy).then_inc(w_hi, 1)
                        else:
                            act.activation(w2_h[:, 0:HT - 1, :], w2_l[:, 0:HT - 1, :], ACT.Copy)
                            act.activation(w2_h[0:HID_LAST, HT - 1, :], w2_l[0:HID_LAST, HT - 1, :], ACT.Copy).then_inc(w_hi, 1)

                    def act_prologue():
                        act.wait_ge(lw_in, b * LW_B + (l + 1) * LW_L)
                        for a in range(3):
                            act.activation(wqkv_h[a][:], wqkv_l[:, :, a * INNER:(a + 1) * INNER], ACT.Copy).then_inc(wa_hi, 1)
                        square(n0)
                        read_values(n0, 0)
                        read_turned(n0, 0)
                        square(n0 + 1)

                    def act_window(i, par, before, next1, next2):
                        n = n0 + i * 2 + par
                        exp_item(n, 0)
                        exp_item(n, 1)
                        if next1:
                            read_turned(n + 1, 1 - par)
                        read_probs(n, 0)
                        read_probs(n, 1)
                        if next2:
                            square(n + 2)
                        act.wait_ge(ol_full, n + 1)
                        act.activation(oL[:].rearrange("p m n -> p (m n)"), psum[:, OL_B, :], ACT.Copy).then_inc(ol_read, 1)
                        if next1:
                            read_values(n + 1, 1 - par)
                        if not next2:
                            split_weights(par)
                    windows(act, act_prologue, act_window)
                    phase_end(act, b, PH_L0 + l * 2)

                    m0, q0 = layer_index(b, l) * CHUNKS, b * LN_B + 2 * CHUNKS + l * CHUNKS

                    def act_norm(c, par):
                        ln_square(act, q0 + c, par)
                        ln_deviation(act, q0 + c, par)

                    def act_chunk(i, par, has_next):
                        for t, (o, size) in enumerate(HID_TILES):
                            k = (m0 + i * 2 + par) * HT + t
                            act.wait_ge(ag_full, k + 1)
                            act.wait_ge(ug_done, k + 1)
                            act.activation(gl[t % 2][0:size, :], psum[0:size, 4 + t % 2, :], ACT.Gelu, bias=vec_b1[0:size, 1, t:t + 1]).then_inc(gelu_done, 1)
                            if has_next and t == NORM_AT:
                                ln_deviation(act, q0 + i * 2 + par + 1, 1 - par)
                            act.wait_ge(ug_done, k + 3)
                            act.wait_ge(down_done, k + 1)
                            act.activation(ug_h[t % 3][0:size, :], uf[t % 2][0:size, :], ACT.Copy).then_inc(ug_hi, 1)
                            if has_next and t == 1:
                                ln_square(act, q0 + i * 2 + par + 1, 1 - par)
                    mlp(act, lambda: act_norm(0, 0), act_chunk)
                    phase_end(act, b, PH_L0 + l * 2 + 1)
                phase_end(act, b, PH_STORE)

        @block.vector
        def _(dve):
            dve.wait_ge(su_p, 1)
            dve.tensor_copy(mod[:], psum[:, 0, 0:12 * B].rearrange("p (j b) -> p j b", b=B)).then_inc(su_d, 1)
            dve.wait_ge(su_d, 1)
            for j0 in (2, 8):
                dve.tensor_scalar(mod[:, j0:j0 + 2, :], mod[:, j0:j0 + 2, :], 1.0, None, ALU.add).then_inc(su_d, 1)
            dve.wait_ge(ld, 16 * 8)
            dve.tensor_tensor(bo_all[:], psum[:, 1, 0:HALVES], bo_t[:], ALU.add).then_inc(su_d, 1)
            gview = mod[:].rearrange("p (g k) b -> p g k b", g=2)[:, :, 4:6, :]
            dve.tensor_scalar(gsign[:], gview, 0.0, 2.0, ALU.is_ge, ALU.mult).then_inc(su_d, 1)
            dve.scalar_tensor_tensor(gsize[:], gview, -1.0, gview, ALU.mult, ALU.max).then_inc(su_d, 1)
            dve.wait_ge(su_d, 6)
            dve.tensor_scalar(gsize[:], gsize[:], 0.25, None, ALU.max).then_inc(su_d, 1)
            dve.wait_ge(su_d, 7)
            dve.scalar_tensor_tensor(gview, gsign[:], -1.0, gsize[:], ALU.add, ALU.mult).then_inc(su_d, 1)
            dve.wait_ge(su_d, 8)
            for s, n in ((ring_free, OFF_RING + 2), (dve_sum, OFF_DVE), (o_free, CP),
                         (ln_c, 1), (ln_done, 2), (ug_done, 2), (y_read, 1), (lo_read, 1)):
                dve.sem_inc(s, n)
            with dve.Fori(0, B) as b:
                phase_end(dve, b, PH_LOAD)
                for s in range(2):
                    dve.memset(kh1[s][DH:DH + 1, :].bitcast(F32), 1.0)
                dve.tensor_copy(modb[:], mod[:, :, bass.ds(b, 1)].rearrange("p j o -> p (j o)")).then_inc(mod_ok, 1)
                dve.wait_ge(mod_ok, b * 2 + 1)
                dve.tensor_tensor(gabo[:], modb[:, 4:6], bo_all[:], ALU.mult).then_inc(mod_ok, 1)
                dve.wait_ge(mod_ok, b * 2 + 2)
                ln_dve(dve, b * LN_B, lambda c: lambda h: hT[:, h, c * T:(c + 1) * T],
                       lambda h: modb[:, 2 + h:3 + h], lambda h: modb[:, h:h + 1])
                for h in range(HALVES):
                    dve.tensor_scalar(xT[:, h, :], xT[:, h, :], gabo[:, h:h + 1], None, ALU.add)
                phase_end(dve, b, PH_LN1)

                def proj_qk(G, s, i):
                    cols = slice(i * T, (i + 1) * T)
                    ps = psum[:, S_BANK + i % 4, :]
                    dve.wait_ge(pj_hi, G * QK_ITEMS + i + 1)
                    dve.tensor_copy(kh1[s][0:DH, cols], klh[s][DH:P, cols])
                    dve.scalar_tensor_tensor(qlm[s][0:DH, cols], ps[0:DH], bqk_h[s][0:DH, 0:1], qhh[s][0:DH, cols], ALU.add, ALU.subtract)
                    dve.scalar_tensor_tensor(klh[s][0:DH, cols], ps[DH:P], bqk_h[s][DH:P, 0:1], klh[s][DH:P, cols], ALU.add, ALU.subtract).then_inc(pj_dve, 1)

                def ring_wait(rb, i):
                    dve.wait_ge(ring_full, OFF_RING + rb + i + 1)
                    return psum[:, M_BANK + i % 2, :]

                def proj_v(rb, r, i):
                    ps = ring_wait(rb, r)
                    dve.tensor_copy(vv[:, i * V_TILES:(i + 1) * V_TILES, :], ps.rearrange("p (t d) -> p t d", d=P)).then_inc(ring_free, 1)

                def max_tile(rb, i, j):
                    ps = ring_wait(rb, i)
                    dve.tensor_reduce(mx4[:, j // CHUNKS, j % CHUNKS:j % CHUNKS + 1], ps, AX_X, ALU.max).then_inc(ring_free, 1)

                def max_all(rb, r):
                    dve.wait_ge(ring_free, OFF_RING + 2 + rb + r)
                    dve.tensor_reduce(mx1[:], mx4[:], AX_X, ALU.max).then_inc(mx_red, 1)

                def max_neg(G, rb, r):
                    ps = ring_wait(rb, r)
                    dve.wait_ge(mrow, G * 16 + 16)
                    dve.tensor_scalar(nmx[:], ps[0:KT, 0:P], -1.0, None, ALU.mult).then_inc(ring_free, 1)

                def add_sum(G, cp, j):
                    kt = SUM_DVE[j]
                    dve.wait_ge(exp_done, G * STEPS + cp * KT + kt + 1)
                    if j:
                        dve.wait_ge(dve_sum, G * (CP * DVE_OPS) + OFF_DVE + cp * DVE_OPS + j)
                        dve.tensor_tensor(acc_d[cp][:], acc_d[cp][:], prob[kt % PRING][:], ALU.add).then_inc(dve_sum, 1)
                    else:
                        dve.tensor_copy(acc_d[cp][:], prob[kt % PRING][:]).then_inc(dve_sum, 1)

                def normalise(G, rb, i, hh, cp):
                    ps = ring_wait(rb, i)
                    dve.reciprocal(rcp[:], ps).then_inc(ring_free, 1)
                    dve.wait_ge(ring_free, OFF_RING + 2 + rb + i + 1)
                    dve.wait_ge(pv_done, G * STEPS + OFF_S + (cp + 1) * KT)
                    for j in range(2):
                        rows = slice(j * DH, (j + 1) * DH)
                        op = dve.tensor_tensor(oT[hh * DH:(hh + 1) * DH, (2 * cp + j) * T:(2 * cp + j + 1) * T],
                                               psum[rows, O_BANK + cp, :], rcp[rows, :], ALU.mult)
                    op.then_inc(o_free, 1)

                def out_tile(rb, i, j):
                    ps = ring_wait(rb, i)
                    c, m = divmod(j, HALVES)
                    xs = xT[:, m, c * T:(c + 1) * T]
                    dve.scalar_tensor_tensor(xs, ps, modb[:, 4 + m:5 + m], xs, ALU.mult, ALU.add).then_inc(ring_free, 1)

                def head(b, hp, hh, plan):
                    G, rb, s = head_index(b, hp, hh), ring_base(b, hp), hh
                    for kind, j, r in plan:
                        if kind == "max":
                            max_tile(rb, r, j)
                            if j == RING_MAX - 1:
                                max_all(rb, r + 1)
                        elif kind == "turn":
                            max_neg(G + 1, rb, r)
                        elif kind == "values":
                            cp, kt = divmod(j, KT)
                            if kt in SUM_DVE:
                                add_sum(G, cp, SUM_DVE.index(kt))
                        elif kind == "sum":
                            normalise(G, rb, r, hh, j)
                        elif kind == "proj_qk":
                            proj_qk(G + 2, s, j)
                        elif kind == "proj_v":
                            proj_v(rb, r, j)
                        elif kind == "out":
                            out_tile(rb, r, j)
                for i in range(QK_ITEMS):
                    proj_qk(head_index(b, 0, 0), 0, i)
                for i in range(V_ITEMS):
                    proj_v(ring_base(b, 0), i, i)
                for i in range(QK_ITEMS):
                    proj_qk(head_index(b, 0, 1), 1, i)
                for qt in range(KT):
                    dve.wait_ge(ring_full, OFF_RING + ring_base(b, 0) + V_ITEMS + (qt + 1) * CHUNKS)
                    dve.tensor_reduce(mx4[:, qt, :], psum[:, 4 * (qt % 2):4 * (qt % 2) + 4, :], AX_X, ALU.max).then_inc(ring_free, CHUNKS)
                max_all(ring_base(b, 0), RING_PRO - 1)
                max_neg(head_index(b, 0, 0), ring_base(b, 0), RING_PRO - 1)
                for hh in range(2):
                    head(b, 0, hh, PLAN[FIRST][hh])
                with dve.Fori(1, PAIRS - 1) as hp:
                    for hh in range(2):
                        head(b, hp, hh, PLAN[MIDDLE][hh])
                for hh in range(2):
                    head(b, PAIRS - 1, hh, PLAN[LAST][hh])
                phase_end(dve, b, PH_ATT)
                ln_dve(dve, b * LN_B + CHUNKS, lambda c: lambda h: xf[:, h, columns(c * T, T)],
                       lambda h: modb[:, 8 + h:9 + h], lambda h: modb[:, 6 + h:7 + h])
                dve.wait_ge(msk_in, b * 16 + 16)
                dve.tensor_copy(mask_b[:], mask_f_view).then_inc(msk_ok, 1)
                dve.wait_ge(msk_ok, b * 2 + 1)
                for z in (xf[:, :, 0:1], x1[:, :, 0:1], q_even[DH:P], q_odd[0:DH],
                          w1_h[:, :, 2 * HID:].bitcast(F32), w1_low[:, :, 2 * HID:].bitcast(F32)):
                    dve.memset(z, 0.0)
                dve.tensor_copy(identb[:], identf[:]).then_inc(msk_ok, 1)
                phase_end(dve, b, PH_LN2)
                with dve.Fori(0, LAYERS) as l:
                    n0 = layer_index(b, l) * WINDOWS
                    def window_input(n, w, par):
                        for h in range(HALVES):
                            op = dve.tensor_scalar(hc_h[par][:, h, :], xf[:, h, columns(w * WIN, WIN, shifted=h)], 1.0, None, ALU.mult)
                        op.then_inc(hc_hi, 1)
                        dve.wait_ge(hc_hi, n + 1)
                        for h in range(HALVES):
                            op = dve.tensor_tensor(hc_l[par][:, h, :], xf[:, h, columns(w * WIN, WIN, shifted=h)], hc_h[par][:, h, :], ALU.subtract)
                        op.then_inc(hc_ok, 1)

                    def rotate_start(n, w):
                        dve.wait_ge(sq_done, n + 1)
                        dve.tensor_reduce(ssq[:], qk_sq[:].rearrange("p (h d) -> p h d", d=DH), AX_X, ALU.add).then_inc(ss_done, 1)
                        dve.wait_ge(ss_done, n * 2 + 1)
                        dve.tensor_scalar(ssc[:], ssq[:], 1e-24, None, ALU.max).then_inc(ss_done, 1)
                        at = bass.ds(w, 1) if not isinstance(w, int) else slice(w, w + 1)
                        qk = psum[:, QK_B:QK_B + 2, :].rearrange("p a (h d) -> p a h d", d=DH)
                        u = qk_u[:].rearrange("p (a h d) -> p a h d", a=2, d=DH)
                        v = qk_w[:].rearrange("p (a h d) -> p a h d", a=2, d=DH)
                        tab = rot_l[:, at].rearrange("p o (a t) d -> p (o a) t d", a=2)
                        for a in range(2):
                            dve.tensor_tensor(u[:, a], qk[:, a], tab[:, a, 0:1, :].broadcast_to([P, LHEADS, DH]), ALU.mult)
                            for o in range(2):
                                dst, src = slice(o * 32, (o + 1) * 32), slice((1 - o) * 32, (2 - o) * 32)
                                op = dve.tensor_tensor(v[:, a, :, dst], qk[:, a, :, src],
                                                       tab[:, a, 1:2, dst].broadcast_to([P, LHEADS, 32]), ALU.mult)
                        op.then_inc(ru_done, 1)

                    def rotate_norm(n):
                        dve.wait_ge(ru_done, n * 2 + 2)
                        dve.wait_ge(rn_done, n + 1)
                        dve.tensor_tensor(qk_w[:].rearrange("p (h d) -> p h d", d=DH), qk_u[:].rearrange("p (h d) -> p h d", d=DH),
                                          rnorm[:].unsqueeze(2).broadcast_to([P, 2 * LHEADS, DH]), ALU.mult).then_inc(rot_done, 1)

                    def item_max(n, it):
                        hs = slice(it * IH, (it + 1) * IH)
                        dve.wait_ge(ls_full, n * ITEMS + it + 1)
                        dve.tensor_reduce(lmax[:, hs], psum[:, 2 * it:2 * it + 2, :].rearrange("p a (h k) -> p (a h) k", k=2 * WIN), AX_X, ALU.max).then_inc(lmx_done, 1)
                        dve.wait_ge(lmx_done, n * ITEMS + it + 1)
                        dve.tensor_scalar(lneg[:, hs], lmax[:, hs], -QK_SCALE, None, ALU.mult).then_inc(lneg_done, 1)

                    def item_rcp(n, it):
                        hs = slice(it * IH, (it + 1) * IH)
                        dve.wait_ge(lexp_done, n * ITEMS + it + 1)
                        dve.reciprocal(lrcp[:, hs], lsum[:, hs]).then_inc(lrcp_done, 1)

                    def dve_prologue():
                        window_input(n0, 0, 0)
                        for a in range(3):
                            dve.wait_ge(wa_hi, layer_index(b, l) * 3 + a + 1)
                            part = slice(a * INNER, (a + 1) * INNER)
                            dve.tensor_tensor(wqkv_low[:, :, part], wqkv_l[:, :, part], wqkv_h[a][:], ALU.subtract).then_inc(wa_lo, 1)
                        window_input(n0 + 1, 1, 1)
                        dve.memset(k_l[:, :, 1, :], 0.0)
                        dve.memset(v_l[1][:], 0.0).then_inc(zp_ok, 1)
                        dve.wait_ge(lw_in, b * LW_B + (l + 1) * LW_L)
                        dve.tensor_tensor(rot_l[:].rearrange("p w t d -> p w (t d)"), rot_l[:].rearrange("p w t d -> p w (t d)"),
                                          scales[:].rearrange("p t d -> p (t d)").unsqueeze(1).broadcast_to([P, WINDOWS, 4 * DH]), ALU.mult).then_inc(rot_ok, 1)
                        dve.wait_ge(rot_ok, layer_index(b, l) + 1)
                        rotate_start(n0, 0)
                        rotate_norm(n0)
                        rotate_start(n0 + 1, 1)

                    def residual(n, w):
                        dve.wait_ge(lo_full, n + 1)
                        cols = columns(w * WIN, WIN)
                        dve.tensor_tensor(x1[:, :, cols], xf[:, :, cols], psum[:, OL_B, 0:HALVES * WIN].rearrange("p (h n) -> p h n", n=WIN), ALU.add).then_inc(lo_read, 1)

                    def dve_window(i, par, before, next1, next2):
                        w = i * 2 + par
                        n = n0 + w
                        item_max(n, 0)
                        item_max(n, 1)
                        item_rcp(n, 0)
                        if next1:
                            rotate_norm(n + 1)
                        if before:
                            residual(n - 1, w - 1)
                        item_rcp(n, 1)
                        if next2:
                            dve.wait_ge(vl_full, n + 1)
                            window_input(n + 2, w + 2, par)
                            rotate_start(n + 2, w + 2)
                        if not next1:
                            residual(n, w)
                    windows(dve, dve_prologue, dve_window)
                    phase_end(dve, b, PH_L0 + l * 2)

                    m0, q0 = layer_index(b, l) * CHUNKS, b * LN_B + 2 * CHUNKS + l * CHUNKS
                    dve.wait_ge(l1_in, (layer_index(b, l) + 1) * (16 * 11))

                    def gain(h):
                        return vec_g[:, h:h + 1]

                    def shift(h):
                        return vec_b[:, h:h + 1]

                    def shifted_src(c):
                        return lambda h: x1[:, h, columns(c * T, T, shifted=h)]

                    def split_norm(m, n, par):
                        for h in range(HALVES):
                            op = dve.tensor_scalar(hn_h[par][:, h, :], lnc[par][:, h, :], shift(h), None, ALU.add)
                        op.then_inc(hn_hi, 1)
                        dve.wait_ge(hn_hi, m + 1)
                        for h in range(HALVES):
                            op = dve.scalar_tensor_tensor(hn_l[par][:, h, :], lnc[par][:, h, :], shift(h), hn_h[par][:, h, :], ALU.add, ALU.subtract)
                        op.then_inc(ln_done, 1)

                    def dve_mlp_prologue():
                        ln_centre(dve, q0, 0, shifted_src(0))
                        ln_inverse(dve, q0, 0)
                        ln_gain(dve, q0, 0, gain)
                        split_norm(m0, q0, 0)

                    def dve_chunk(i, par, has_next):
                        c = i * 2 + par
                        m = m0 + c
                        for t, (o, size) in enumerate(HID_TILES):
                            k = m * HT + t
                            if has_next and t == 1:
                                ln_centre(dve, q0 + c + 1, 1 - par, shifted_src(c + 1))
                            dve.wait_ge(gelu_done, k + 1)
                            dve.wait_ge(ug_lo, k + 1)
                            dve.scalar_tensor_tensor(uf[t % 2][0:size, :], psum[0:size, 2 + t % 2, :], vec_b1[0:size, 0, t:t + 1], gl[t % 2][0:size, :],
                                                     ALU.add, ALU.mult).then_inc(ug_done, 1)
                            if has_next and t == NORM_AT:
                                ln_inverse(dve, q0 + c + 1, 1 - par)
                            if has_next and t == NORM_AT + 1:
                                ln_gain(dve, q0 + c + 1, 1 - par, gain)
                                split_norm(m + 1, q0 + c + 1, 1 - par)
                        dve.wait_ge(down_done, (m + 1) * HT + 3)
                        for h in range(HALVES):
                            op = dve.scalar_tensor_tensor(xf[:, h, columns(c * T, T)], psum[:, 6 + h, :], vec_b2[:, h:h + 1], x1[:, h, columns(c * T, T)], ALU.add, ALU.add)
                        op.then_inc(y_read, 1)
                    mlp(dve, dve_mlp_prologue, dve_chunk)
                    phase_end(dve, b, PH_L0 + l * 2 + 1)
                for h in range(HALVES):
                    op = dve.scalar_tensor_tensor(xT[:, h, :], xf[:, h, 1:N + 1], modb[:, 10 + h:11 + h], xT[:, h, :], ALU.mult, ALU.add)
                op.then_inc(fin_ok, 1)
                for t in range(KT):
                    dve.wait_ge(ot_full, b * KT + t + 1)
                    if t >= 4:
                        dve.wait_ge(stored[t % 4], b * (4 * KT) + 16 * (t // 4))
                    dve.tensor_copy(tok[t % 4][:], psum[:, t % 4, 0:D]).then_inc(ot_tok, 1)
                phase_end(dve, b, PH_STORE)

        @block.tensor
        def _(pe):
            pe.wait_ge(su_a, 1)
            pe.wait_ge(ld, 16 * 8)
            for j in range(12):
                for h in range(HALVES):
                    mm = pe.matmul(psum[:, 0, j * B:(j + 1) * B], wmod_sb[:, h, j * P:(j + 1) * P], csil[:, h, :],
                                   start=(h == 0), stop=(h == HALVES - 1))
            for m in range(HALVES):
                for k in range(PAIRS):
                    wo_k = prob[k // 4][:, (k % 4) * D + m * P:(k % 4) * D + (m + 1) * P]
                    mm = pe.matmul(psum[:, 1, m:m + 1], wo_k, bv_t[:, k:k + 1], start=(k == 0), stop=(k == PAIRS - 1))
            mm.then_inc(su_p, 1)
            pe.wait_ge(cst, 2)
            pe.wait_ge(su_d, 8)
            pe.sem_inc(ring_full, OFF_RING)
            pe.sem_inc(pv_done, OFF_S)
            pe.sem_inc(ln_var, 2)
            pe.sem_inc(down_done, 3)
            with pe.Fori(0, B) as b:
                for t in range(KT):
                    pe.wait_ge(x_in[t % 4], b * (16 * (KT // 4)) + 16 * (t // 4 + 1))
                    if t >= 4:
                        pe.wait_ge(tp_free, b * KT + t - 3)
                    for h in range(HALVES):
                        mm = pe.transpose(psum[:, t % 4, h * P:(h + 1) * P], tok[t % 4][:, h * P:(h + 1) * P], identf[:])
                    mm.then_inc(tp_full, 1)
                phase_end(pe, b, PH_LOAD)
                ln_pe(pe, b * LN_B)
                phase_end(pe, b, PH_LN1)

                def ring_slot(rb, r):
                    pe.wait_ge(ring_free, OFF_RING + rb + r + 1)
                    return psum[:, M_BANK + r % 2, :]

                def proj_qk(G, s, i, use):
                    if i == 0:
                        pe.wait_ge(w_in[s], 64 * use)
                    for h in range(HALVES):
                        mm = pe.matmul(psum[:, S_BANK + i, :], wqk_h[s][:, h, :], hT[:, h, i * T:(i + 1) * T],
                                       start=(h == 0), stop=(h == HALVES - 1))
                    mm.then_inc(pj_full, 1)

                def proj_v(rb, r, i, use):
                    ps = ring_slot(rb, r)
                    if i == 0:
                        pe.wait_ge(wv_in, 16 * use)
                    for t in range(V_TILES):
                        tt = i * V_TILES + t
                        for h in range(HALVES):
                            mm = pe.matmul(ps[:, t * P:(t + 1) * P], hT[:, h, tt * P:(tt + 1) * P], wv_p[:, h, :],
                                           start=(h == 0), stop=(h == HALVES - 1))
                    mm.then_inc(ring_full, 1)

                def max_tile(rb, r, s, j):
                    qt, c = divmod(j, CHUNKS)
                    ps = ring_slot(rb, r)
                    pe.matmul(ps, qhh[s][0:DH, qt * P:(qt + 1) * P], kh1[s][0:DH, c * T:(c + 1) * T],
                              start=True, stop=True).then_inc(ring_full, 1)

                def turn(G, rb, r):
                    ps = ring_slot(rb, r)
                    pe.wait_ge(mx_red, G + 1)
                    pe.transpose(ps[0:KT, 0:P], mx1[:], identf[:]).then_inc(ring_full, 1)

                def projected(G, items):
                    pe.wait_ge(pj_dup, G * QK_ITEMS + items)
                    pe.wait_ge(pj_dve, G * QK_ITEMS + items)

                def scores(G, s, t):
                    cp, kt = divmod(t, KT)
                    if t >= 2:
                        pe.wait_ge(exp_done, G * STEPS + t - 1)
                    keys = slice(kt * P, (kt + 1) * P)
                    for j in range(2):
                        cols = slice((2 * cp + j) * T, (2 * cp + j + 1) * T)
                        ps = psum[:, S_BANK + 2 * (t % 2) + j, :]
                        pe.matmul(ps, klh[s][:, keys], qhh[s][:, cols], start=True, stop=False)
                        mm = pe.matmul(ps, kh1[s][:, keys], qlm[s][:, cols], start=False, stop=True)
                    mm.then_inc(s_full, 1)

                def values(G, rb, s, t):
                    cp, kt = divmod(t, KT)
                    if s == 0 and t == 0:
                        pe.wait_ge(ring_free, OFF_RING + 2 + rb + VALUES_READ)
                    pe.wait_ge(exp_done, G * STEPS + t + 1)
                    if kt == 0:
                        pe.wait_ge(o_free, G * CP + cp + 1)
                    for j in range(2):
                        mm = pe.matmul(psum[j * DH:(j + 1) * DH, O_BANK + cp, :], vv[:, kt, s * DH:(s + 1) * DH],
                                       prob[t % PRING][:, j * T:(j + 1) * T], start=(kt == 0), stop=(kt == KT - 1))
                    mm.then_inc(pv_done, 1)

                def sums(G, rb, r, cp):
                    ps = ring_slot(rb, r)
                    pe.wait_ge(pool_sum, G * (CP * POOL_OPS) + OFF_POOL + (cp + 1) * POOL_OPS)
                    for j in range(2):
                        mm = pe.matmul(ps[j * DH:(j + 1) * DH], ones[:], acc_p[cp][:, j * T:(j + 1) * T], start=True, stop=True)
                    mm.then_inc(ring_full, 1)

                def out_tile(G, rb, r, j, use):
                    c, m = divmod(j, HALVES)
                    ps = ring_slot(rb, r)
                    if j == 0:
                        pe.wait_ge(wo_in, 16 * use)
                        pe.wait_ge(o_free, G * CP + CP + CP)
                    pe.matmul(ps, wo_p[:, m * P:(m + 1) * P], oT[:, c * T:(c + 1) * T], start=True, stop=True).then_inc(ring_full, 1)

                def head(b, hp, hh, which):
                    G, rb, s = head_index(b, hp, hh), ring_base(b, hp), hh
                    tail = which == LAST and hh == 1
                    pe.wait_ge(mrow, G * 16 + 32)
                    for kind, j, r in PLAN[which][hh]:
                        if kind == "scores":
                            if j < 2 and not tail:
                                projected(G + 1, 2 * j + 2)
                            scores(G, s, j)
                        elif kind == "max":
                            max_tile(rb, r, 1 - s, j)
                        elif kind == "values":
                            values(G, rb, s, j)
                        elif kind == "sum":
                            sums(G, rb, r, j)
                        elif kind == "turn":
                            turn(G + 1, rb, r)
                        elif kind == "proj_qk":
                            if j % 2 == 0:
                                pe.wait_ge(exp_done, G * STEPS + STEPS - 1 + j // 2)
                            proj_qk(G + 2, s, j, b * PAIRS + hp + 2)
                        elif kind == "proj_v":
                            proj_v(rb, r, j, b * PAIRS + hp + 2)
                        elif kind == "out":
                            if tail:
                                out_tile(G, rb, r, j, b * PAIRS + hp + 1)
                            else:
                                out_tile(G - 1, rb, r, j, b * PAIRS + hp)
                for i in range(QK_ITEMS):
                    proj_qk(head_index(b, 0, 0), 0, i, b * PAIRS + 1)
                for i in range(V_ITEMS):
                    proj_v(ring_base(b, 0), i, i, b * PAIRS + 1)
                projected(head_index(b, 0, 0), QK_ITEMS)
                for i in range(QK_ITEMS):
                    proj_qk(head_index(b, 0, 1), 1, i, b * PAIRS + 1)
                projected(head_index(b, 0, 1), QK_ITEMS)
                for qt in range(KT):
                    pe.wait_ge(ring_free, OFF_RING + 2 + ring_base(b, 0) + V_ITEMS + max(qt - 1, 0) * CHUNKS)
                    for c in range(CHUNKS):
                        mm = pe.matmul(psum[:, 4 * (qt % 2) + c, :], qhh[0][0:DH, qt * P:(qt + 1) * P], kh1[0][0:DH, c * T:(c + 1) * T],
                                       start=True, stop=True)
                    mm.then_inc(ring_full, CHUNKS)
                turn(head_index(b, 0, 0), ring_base(b, 0), RING_PRO - 1)
                pe.sem_inc(bar_left, 1)
                for hh in range(2):
                    head(b, 0, hh, FIRST)
                with pe.Fori(1, PAIRS - 1) as hp:
                    for hh in range(2):
                        head(b, hp, hh, MIDDLE)
                for hh in range(2):
                    head(b, PAIRS - 1, hh, LAST)
                phase_end(pe, b, PH_ATT)
                ln_pe(pe, b * LN_B + CHUNKS)
                phase_end(pe, b, PH_LN2)
                with pe.Fori(0, LAYERS) as l:
                    n0 = layer_index(b, l) * WINDOWS
                    pe.wait_ge(lw_in, b * LW_B + (l + 1) * LW_L)
                    pe.wait_ge(msk_ok, b * 2 + 2)

                    def project(dst, par, a):
                        for h in range(HALVES):
                            high, low = wqkv_h[a][:, h, :], wqkv_low[:, h, a * INNER:(a + 1) * INNER]
                            for i, (x_part, w_part) in enumerate(((hc_h, high), (hc_h, low), (hc_l, high))):
                                mm = pe.matmul(dst, x_part[par][:, h, :], w_part, start=(h == 0 and i == 0), stop=(h == HALVES - 1 and i == 2))
                        return mm

                    def project_qk(n, par):
                        pe.wait_ge(hc_ok, n + 1)
                        pe.wait_ge(qkT_read, n + 1)
                        for a in range(2):
                            mm = project(psum[:, QK_B + a, :], par, a)
                        mm.then_inc(qk_full, 1)

                    def project_v(n, par):
                        pe.wait_ge(vl_read, n + 1)
                        mm = project(psum[:, V_B, :], par, 2)
                        mm.then_inc(vl_full, 1)

                    def turn_qk(n):
                        pe.wait_ge(rot_done, n + 1)
                        for a in range(2):
                            for p in range(LPAIRS):
                                mm = pe.transpose(psum[:, QK_B + a, p * WIN:(p + 1) * WIN], qk_w[:, a * INNER + p * P:a * INNER + (p + 1) * P], identf[:])
                        mm.then_inc(qkT_full, 1)

                    def local_scores(n, i, par, it):
                        if it == 0:
                            pe.wait_ge(qkT_read, n + 2)
                        pe.wait_ge(lpT_read, n * ITEMS + it + 1)
                        for a in range(2):
                            p = 2 * it + a
                            ps = psum[:, p, :]
                            if par:
                                mask = mask_b[:, WINDOWS // 2:WINDOWS // 2 + 1, :]
                            else:
                                mask = mask_b[:, (slice(i, i + 1) if isinstance(i, int) else bass.ds(i, 1)), :]
                            pe.matmul(ps.rearrange("p (t k) -> p t k", t=2), identb[:], mask.broadcast_to([P, 2, 2 * WIN]),
                                      start=True, stop=False, skip_group_check=True)
                            for o, q in enumerate((q_even, q_odd)):
                                mm = pe.matmul(ps[:, o * 2 * WIN:(o + 1) * 2 * WIN], q[:, p, :], k_l[:, p].rearrange("p s n -> p (s n)"),
                                               start=False, stop=True, skip_group_check=True)
                        mm.then_inc(ls_full, 1)

                    def turn_probs(n, it):
                        pe.wait_ge(lp_done, n * ITEMS + it + 1)
                        for h in range(IH):
                            for half in range(2):
                                j = h * 2 + half
                                mm = pe.transpose(psum[:, 2 * it + j // 4, (j % 4) * P:(j % 4 + 1) * P], lp[:, it * IH + h, half * WIN:(half + 1) * WIN], identf[:])
                        mm.then_inc(lpT_full, 1)

                    def local_values(n, par, it):
                        pe.wait_ge(lpT_read, n * ITEMS + it + 1 + ITEMS)
                        if it == 0:
                            pe.wait_ge(lo_read, n + 1)
                        for p in range(2 * it, 2 * it + 2):
                            for half in range(2):
                                for o in range(2):
                                    h = 2 * p + o
                                    mm = pe.matmul(psum[o * DH:(o + 1) * DH, OL_B, p * WIN:(p + 1) * WIN], v_l[half][:, h * DH:(h + 1) * DH], lpT[:, h, half, :],
                                                   start=(half == 0), stop=(half == 1), skip_group_check=True)
                        if it == 1:
                            mm.then_inc(ol_full, 1)

                    def local_out(n):
                        pe.wait_ge(ol_read, n + 1)
                        for m in range(HALVES):
                            for k in range(LPAIRS):
                                mm = pe.matmul(psum[:, OL_B, m * WIN:(m + 1) * WIN], wo_l[:, k, m * P:(m + 1) * P], oL[:, k, :],
                                               start=(k == 0), stop=(k == LPAIRS - 1))
                        mm.then_inc(lo_full, 1)

                    def pe_prologue():
                        pe.wait_ge(wa_lo, (layer_index(b, l) + 1) * 3)
                        project_qk(n0, 0)
                        project_v(n0, 0)
                        turn_qk(n0)
                        project_qk(n0 + 1, 1)
                        pe.wait_ge(zp_ok, layer_index(b, l) + 1)

                    def pe_window(i, par, before, next1, next2):
                        n = n0 + i * 2 + par
                        local_scores(n, i, par, 0)
                        local_scores(n, i, par, 1)
                        if before:
                            local_out(n - 1)
                        if next1:
                            project_v(n + 1, 1 - par)
                            turn_qk(n + 1)
                        turn_probs(n, 0)
                        turn_probs(n, 1)
                        if next2:
                            project_qk(n + 2, par)
                        local_values(n, par, 0)
                        local_values(n, par, 1)
                        if not next1:
                            local_out(n)
                    windows(pe, pe_prologue, pe_window)
                    phase_end(pe, b, PH_L0 + l * 2)

                    m0, q0 = layer_index(b, l) * CHUNKS, b * LN_B + 2 * CHUNKS + l * CHUNKS
                    pe.wait_ge(l1_in, (layer_index(b, l) + 1) * (16 * 11))

                    def shifted_src(c):
                        return lambda h: x1[:, h, columns(c * T, T, shifted=h)]

                    def pe_mlp_prologue():
                        ln_mean(pe, q0, shifted_src(0))
                        ln_variance(pe, q0, 0)

                    def up(m, n, par, t):
                        if t == 0:
                            pe.wait_ge(ln_done, n + 3)
                        pe.wait_ge(ug_done, m * HT + t + 1)
                        for j, bank in ((0, 2 + t % 2), (1, 4 + t % 2)):
                            for h in range(HALVES):
                                cols = slice(j * HID + t * P, j * HID + (t + 1) * P)
                                high, low = w1_h[:, h, cols], w1_low[:, h, cols]
                                for a, (w, src) in enumerate(((high, hn_h), (low, hn_h), (high, hn_l))):
                                    mm = pe.matmul(psum[:, bank, :], w, src[par][:, h, :],
                                                   start=(h == 0 and a == 0), stop=(h == HALVES - 1 and a == 2))
                        mm.then_inc(ag_full, 1)

                    def down(m, t):
                        size = HID_TILES[t][1]
                        pe.wait_ge(ug_lo, m * HT + t + 3)
                        if t == 0:
                            pe.wait_ge(y_read, m + 1)
                        for h in range(HALVES):
                            cols = slice(h * P, (h + 1) * P)
                            high, low = w2_h[0:size, t, cols], w2_low[0:size, t, cols]
                            for a, (w, src) in enumerate(((high, ug_h), (low, ug_h), (high, ug_l))):
                                mm = pe.matmul(psum[:, 6 + h, :], w, src[t % 3][0:size, :],
                                               start=(t == 0 and a == 0), stop=(t == HT - 1 and a == 2))
                        mm.then_inc(down_done, 1)

                    def pe_mlp_prologue():
                        ln_mean(pe, q0, shifted_src(0))
                        ln_variance(pe, q0, 0)
                        pe.wait_ge(w_lo, (layer_index(b, l) + 1) * 3)
                        up(m0, q0, 0, 0)

                    def pe_chunk(i, par, has_next):
                        c = i * 2 + par
                        m = m0 + c
                        for t in range(1, HT):
                            up(m, q0 + c, par, t)
                            if t >= 2:
                                down(m, t - 2)
                            if has_next and t == 1:
                                ln_mean(pe, q0 + c + 1, shifted_src(c + 1))
                            if has_next and t == NORM_AT - 1:
                                ln_variance(pe, q0 + c + 1, 1 - par)
                        down(m, HT - 2)
                        if has_next:
                            up(m + 1, q0 + c + 1, 1 - par, 0)
                        down(m, HT - 1)
                    mlp(pe, pe_mlp_prologue, pe_chunk)
                    phase_end(pe, b, PH_L0 + l * 2 + 1)
                pe.wait_ge(fin_ok, b + 1)
                for t in range(KT):
                    if t >= 4:
                        pe.wait_ge(ot_tok, b * KT + t - 3)
                    for h in range(HALVES):
                        mm = pe.transpose(psum[:, t % 4, h * P:(h + 1) * P], xT[:, h, t * P:(t + 1) * P], identf[:])
                    mm.then_inc(ot_full, 1)
                phase_end(pe, b, PH_STORE)


_INS = ["L0_attn_x", "L0_attn_Wq", "L0_attn_bq", "L0_attn_Wk", "L0_attn_bk", "L0_attn_Wv", "L0_attn_bv", "L0_attn_Wo",
        "L0_attn_bo", "L0_ffn_wqkv", "L0_ffn_q_scale", "L0_ffn_k_scale", "L0_ffn_wo", "L0_ffn_ln_g", "L0_ffn_ln_b",
        "L0_ffn_w1", "L0_ffn_b1", "L0_ffn_w2", "L0_ffn_b2", "L0_c", "L0_wmod"]


def kernel(**inputs):
    import concourse.bacc as bacc
    from concourse.bass_utils import run_bass_kernel_spmd

    nc = bacc.Bacc("TRN2", target_bir_lowering=False, num_devices=1)
    arrays = {n: np.ascontiguousarray(inputs[n]) for n in _INS}
    arrays.update({"const_" + n: a for n, a in shape_constants().items()})
    args = [nc.dram_tensor(n, a.shape, mybir.dt.from_np(a.dtype), kind="ExternalInput").ap() for n, a in arrays.items()]
    out = nc.dram_tensor("out", (B, N, D), F32, kind="ExternalOutput").ap()
    adaln_block(nc, *args, out)
    r = run_bass_kernel_spmd(nc, [arrays], core_ids=[0])
    return r.results[0]["out"]
```
